# Optimizing a Trainium2 kernel written in Bass

```python
import numpy as np
import jax
import jax.numpy as jnp

def _softmax(x, axis=-1):
    return jax.nn.softmax(x, axis=axis)

def _gelu(x):
    return jax.nn.gelu(x, approximate=True)

def _silu(x):
    return jax.nn.silu(x)

def _sigmoid(x):
    return jax.nn.sigmoid(x)

def _layernorm(x, axis=-1, eps=1e-05):
    m = jnp.mean(x, axis=axis, keepdims=True)
    v = jnp.var(x, axis=axis, keepdims=True)
    return (x - m) / jnp.sqrt(v + eps)

def _scatter_add(tgt, idx, src, axis=0):
    return tgt.at[idx].add(src)

def _segment_sum(src, seg, n):
    return jax.ops.segment_sum(src, seg, n)
kernel_name = 'mk_macaron_d1_jaxref_r8_457fb9'

def setup_inputs(seed: int=0):
    np.random.seed(seed)
    _w = jnp.asarray

    def _L0_attn_setup():
        import jax, jax.numpy as jnp
        import numpy as np
        D_MODEL = 128
        NUM_HEADS = 16
        HEAD_DIM = D_MODEL // NUM_HEADS
        LN_EPS = 1e-05

        def _layernorm(x, gamma, beta):
            mu = jnp.mean(x, axis=-1, keepdims=True)
            var = jnp.mean(jnp.square(x - mu), axis=-1, keepdims=True)
            return (x - mu) * jax.lax.rsqrt(var + LN_EPS) * gamma + beta
        key = jax.random.key(seed)
        ks = jax.random.split(key, 7)
        B, S, D = (2, 256, D_MODEL)
        x = jax.random.normal(ks[0], (B, S, D), dtype=jnp.float32)
        lim1 = 1.0 / np.sqrt(D)
        W1 = jax.random.uniform(ks[1], (D, 4 * D), minval=-lim1, maxval=lim1, dtype=jnp.float32)
        b1 = jax.random.uniform(ks[2], (4 * D,), minval=-lim1, maxval=lim1, dtype=jnp.float32)
        W2 = jax.random.uniform(ks[3], (D, D), minval=-lim1, maxval=lim1, dtype=jnp.float32)
        b2 = jax.random.uniform(ks[4], (D,), minval=-lim1, maxval=lim1, dtype=jnp.float32)
        gamma = jnp.ones((D,), dtype=jnp.float32)
        beta = jnp.zeros((D,), dtype=jnp.float32)
        return {'x': x, 'W1': W1, 'b1': b1, 'W2': W2, 'b2': b2, 'gamma': gamma, 'beta': beta}
    _L0_attn_in = _L0_attn_setup()

    def _L0_ffn_setup():
        import jax, jax.numpy as jnp
        import numpy as np
        D_MODEL = 128
        D_FF = 512
        NUM_EXPERTS = 8
        TOP_K = 2
        B, S = (4, 512)
        key = jax.random.key(seed)
        ks = jax.random.split(key, 7)
        s_dm = 1.0 / np.sqrt(D_MODEL)
        s_ff = 1.0 / np.sqrt(D_FF)
        return {'x': jax.random.normal(ks[0], (B, S, D_MODEL), jnp.float32), 'router_w': jax.random.normal(ks[1], (D_MODEL, NUM_EXPERTS), jnp.float32) * s_dm, 'router_b': jnp.zeros((NUM_EXPERTS,), jnp.float32), 'w1': jax.random.normal(ks[2], (NUM_EXPERTS, D_MODEL, D_FF), jnp.float32) * s_dm, 'b1': jnp.zeros((NUM_EXPERTS, D_FF), jnp.float32), 'w2': jax.random.normal(ks[3], (NUM_EXPERTS, D_FF, D_MODEL), jnp.float32) * s_ff, 'b2': jnp.zeros((NUM_EXPERTS, D_MODEL), jnp.float32)}
    _L0_ffn_in = _L0_ffn_setup()
    _d = {'L0_attn_x': _L0_attn_in['x'], 'L0_attn_W1': _L0_attn_in['W1'], 'L0_attn_b1': _L0_attn_in['b1'], 'L0_attn_W2': _L0_attn_in['W2'], 'L0_attn_b2': _L0_attn_in['b2'], 'L0_attn_gamma': _L0_attn_in['gamma'], 'L0_attn_beta': _L0_attn_in['beta'], 'L0_ffn_router_w': _L0_ffn_in['router_w'], 'L0_ffn_router_b': _L0_ffn_in['router_b'], 'L0_ffn_w1': _L0_ffn_in['w1'], 'L0_ffn_b1': _L0_ffn_in['b1'], 'L0_ffn_w2': _L0_ffn_in['w2'], 'L0_ffn_b2': _L0_ffn_in['b2']}
    _x0 = _d['L0_attn_x']
    _d['L0_attn_x'] = jax.random.normal(jax.random.fold_in(jax.random.key(seed), 1), (8, 256, 128), dtype=_x0.dtype)
    del _x0
    return _d

def reference(L0_attn_x, L0_attn_W1, L0_attn_b1, L0_attn_W2, L0_attn_b2, L0_attn_gamma, L0_attn_beta, L0_ffn_router_w, L0_ffn_router_b, L0_ffn_w1, L0_ffn_b1, L0_ffn_w2, L0_ffn_b2):

    def _L0_attn_ref(x, W1, b1, W2, b2, gamma, beta):
        import jax, jax.numpy as jnp
        import numpy as np
        D_MODEL = 128
        NUM_HEADS = 16
        HEAD_DIM = D_MODEL // NUM_HEADS
        LN_EPS = 1e-05

        def _layernorm(x, gamma, beta):
            mu = jnp.mean(x, axis=-1, keepdims=True)
            var = jnp.mean(jnp.square(x - mu), axis=-1, keepdims=True)
            return (x - mu) * jax.lax.rsqrt(var + LN_EPS) * gamma + beta
        B, S, D = x.shape
        H, Dh = (NUM_HEADS, HEAD_DIM)
        x_proj = jax.nn.silu(x @ W1 + b1)
        u, v, q, k = jnp.split(x_proj, 4, axis=-1)
        qh = q.reshape(B, S, H, Dh)
        kh = k.reshape(B, S, H, Dh)
        vh = v.reshape(B, S, H, Dh)
        scores = jnp.einsum('bqhd,bkhd->bhqk', qh, kh)
        attn = jax.nn.silu(scores) / S
        av = jnp.einsum('bhqk,bkhd->bqhd', attn, vh).reshape(B, S, D)
        y = _layernorm(av * u, gamma, beta) @ W2 + b2
        return y

    def _L0_ffn_ref(x, router_w, router_b, w1, b1, w2, b2):
        import jax, jax.numpy as jnp
        import numpy as np
        D_MODEL = 128
        D_FF = 512
        NUM_EXPERTS = 8
        TOP_K = 2
        B, S = (4, 512)
        Bx, Sx, D = x.shape
        xf = x.reshape(-1, D)
        logits = xf @ router_w + router_b
        top_w, sel = jax.lax.top_k(logits, TOP_K)
        gates = jax.nn.softmax(top_w, axis=-1)

        def body(i, acc):
            h = jax.nn.gelu(xf @ w1[i] + b1[i], approximate=False)
            out_i = h @ w2[i] + b2[i]
            gate_i = jnp.sum(gates * (sel == i), axis=-1, keepdims=True)
            return acc + out_i * gate_i
        out = jax.lax.fori_loop(0, NUM_EXPERTS, body, jnp.zeros_like(xf))
        return out.reshape(Bx, Sx, D)
    x = L0_attn_x
    x = x + 0.5 * _L0_ffn_ref(_layernorm(x, axis=-1), L0_ffn_router_w, L0_ffn_router_b, L0_ffn_w1, L0_ffn_b1, L0_ffn_w2, L0_ffn_b2)
    x = x + _L0_attn_ref(_layernorm(x, axis=-1), L0_attn_W1, L0_attn_b1, L0_attn_W2, L0_attn_b2, L0_attn_gamma, L0_attn_beta)
    x = x + 0.5 * _L0_ffn_ref(_layernorm(x, axis=-1), L0_ffn_router_w, L0_ffn_router_b, L0_ffn_w1, L0_ffn_b1, L0_ffn_w2, L0_ffn_b2)
    return x

_drawn_inputs = setup_inputs


def setup_inputs(seed=0):
    import zlib

    import numpy as np

    out = dict(_drawn_inputs(seed))
    spreads = {'L0_attn_gamma': (1.0, 0.2),
     'L0_attn_beta': (0.0, 0.1),
     'L0_ffn_router_b': (0.0, 0.1),
     'L0_ffn_b1': (0.0, 0.1),
     'L0_ffn_b2': (0.0, 0.1)}
    factors = {}
    for name, (base, spread) in spreads.items():
        noise = np.random.default_rng([zlib.crc32(name.encode()), seed]).standard_normal(out[name].shape)
        drawn = base * np.exp(spread * noise) if base else spread * noise
        out[name] = jnp.asarray(drawn.astype(out[name].dtype))
    for name, factor in factors.items():
        out[name] = (out[name] * factor).astype(out[name].dtype)
    return out
```

```python
from contextlib import ExitStack

import numpy as np

import concourse.bass as bass
from concourse import mybir

F32 = mybir.dt.float32
F32R = mybir.dt.float32r
F16 = mybir.dt.float16
BF16 = mybir.dt.bfloat16
I32 = mybir.dt.int32
U32 = mybir.dt.uint32
ALU = mybir.AluOpType
ACT = mybir.ActivationFunctionType
AX = mybir.AxisListType

P = 128
D = 128
BATCH, SEQ = 8, 256
TOKENS = BATCH * SEQ
TILES = TOKENS // P
TPB = SEQ // P
HEADS, HD = 16, 8
HG = 4
GROUPS = HEADS // HG
REP = 4
EXPERTS, FF = 8, 512
CHUNKS = FF // P
TOPK = 2
SLOT_TILES = 40
RING = 4
AHEAD = 5
EPS = 1e-5
RSQRT_SEED = 0x5F3759DF
C_W1, C_W2, C_B1, C_B2 = 0, FF, 2 * FF, 2 * FF + CHUNKS
RECORD = C_B2 + D


class Steps:

    def __init__(self, engine, semaphore):
        self.engine, self.semaphore, self.count, self.turn = engine, semaphore, 0, 0

    def done(self, instruction):
        instruction.then_inc(self.semaphore, 1)
        self.count += 1
        self.engine.wait_ge(self.semaphore, self.turn + self.count)

    def enter(self, i, per_turn):
        self.turn, self.start, self.per_turn = i * per_turn, self.count, per_turn

    def leave(self, turns):
        assert self.count - self.start == self.per_turn, (self.count - self.start, self.per_turn)
        self.count, self.turn = self.start + turns * self.per_turn, 0


def wait(engine, semaphore, value):
    if not isinstance(value, int) or value > 0:
        engine.wait_ge(semaphore, value)


def macaron(nc, x, W1, b1, W2, b2, gamma, beta, router_w, router_b, w1, fb1, w2, fb2, out):
    ctx = ExitStack()
    with ctx:
        def sb(name, shape, dt=F32):
            return ctx.enter_context(nc.sbuf_tensor(name, shape, dt))

        def sem(name):
            return ctx.enter_context(nc.semaphore(name))

        xn_rows = nc.dram_tensor("xn_rows", [TOKENS, D], F32).ap()
        y_rows = nc.dram_tensor("y_rows", [TOPK * TOKENS + SLOT_TILES * P, D], F32).ap()

        ident = sb("ident", [P, P])
        ones = sb("ones", [P, P])
        ones_h = sb("ones_h", [P, P], BF16)
        before = sb("before", [P, P], BF16)
        iota = sb("iota", [P, P])
        token_id = sb("token_id", [P, TILES])
        rank_of = sb("rank_of", [P, EXPERTS])
        spare_row = sb("spare_row", [P, SLOT_TILES])
        quarter = sb("quarter", [P, HG])
        ones8 = sb("ones8", [P, EXPERTS])
        records = sb("records", [P, EXPERTS, RECORD])
        row = sb("row", [1, EXPERTS * D + EXPERTS + 2 * D + D])
        rw = sb("rw", [P, EXPERTS])
        rb_all = sb("rb_all", [P, EXPERTS])
        uvb_all = sb("uvb_all", [P, 2 * D])
        w_in = sb("w_in", [P, 4 * D])
        w_in_hi = sb("w_in_hi", [P, 4 * D], F32R)
        w_in_lo = sb("w_in_lo", [P, 4 * D], F32R)
        w_out = sb("w_out", [P, D])
        w_out_g = sb("w_out_g", [P, D])
        cols = sb("cols", [P, 6])
        beta_all = sb("beta_all", [P, P])
        yb_all = sb("yb_all", [P, D])
        spread = sb("spread", [P, 4, GROUPS, P], F32R)

        X = sb("X", [P, TILES, D])
        stats = sb("stats", [P, TILES, 6])
        mean = sb("mean", [P, TILES])
        rstd = sb("rstd", [P, TILES])
        scr = [sb(f"scr{i}", [P, TILES]) for i in range(5)]

        XNs = sb("XNs", [P, RING, D])
        XTr = sb("XTr", [P, 2, P])
        LG = sb("LG", [P, TILES, EXPERTS])
        one_hot = sb("one_hot", [P, TOPK, TILES, EXPERTS])
        weighed = sb("weighed", [P, TILES, EXPERTS])
        top = sb("top", [P, TOPK, TILES])
        first = sb("first", [P, TILES])
        half_gate = sb("half_gate", [P, TOPK, TILES])
        chosen = sb("chosen", [P, TILES, EXPERTS], BF16)
        run = [sb(f"run{i}", [P, TILES, EXPERTS]) for i in range(2)]
        place = sb("place", [P, TILES, EXPERTS])
        n_int = sb("n_int", [P, EXPERTS], I32)
        n_tiles = sb("n_tiles", [P, EXPERTS])
        n_upto = sb("n_upto", [P, EXPERTS])
        base = sb("base", [P, EXPERTS])
        te_cmp = sb("te_cmp", [1, SLOT_TILES, EXPERTS])
        te_sum = sb("te_sum", [1, SLOT_TILES])
        tile_expert = sb("tile_expert", [1, SLOT_TILES], I32)
        slot_i = sb("slot_i", [P, TOPK * TILES], I32)
        slot_lo_i = sb("slot_lo_i", [P, TOPK * TILES], I32)
        slot_hi_i = sb("slot_hi_i", [P, TOPK * TILES], I32)
        slot_f = sb("slot_f", [P, TOPK * TILES])
        slot_lo = sb("slot_lo", [P, TOPK * TILES])
        slot_hi = sb("slot_hi", [P, TOPK * TILES])
        region = sb("region", [P, TILES * TOPK * D])
        YL = region[:].rearrange("p (t j d) -> p t j d", j=TOPK, d=D)
        A = region[:].rearrange("p (n j q) -> p n j q", j=HG, q=SEQ)
        halves, N = region[:].bitcast(F16), TOPK * TILES
        in_tile = halves[:, 0:N * P].rearrange("p (n s) -> p n s", n=N)
        tile_hot = halves[:, N * P:N * (P + SLOT_TILES)].rearrange("p (n s) -> p n s", n=N)
        tile_load = halves[:, N * (P + SLOT_TILES):N * (P + 3 * SLOT_TILES)].rearrange(
            "p (n a s) -> p n a s", n=N, a=2)
        slot_map = sb("slot_map", [P, 2, SLOT_TILES])
        dst_f = sb("dst_f", [P, SLOT_TILES])
        src_row = sb("src_row", [P, SLOT_TILES], U32)
        dst_row = sb("dst_row", [P, SLOT_TILES], U32)

        src_s = [sb(f"src_s{k}", [P, 1], U32) for k in range(RING)]
        dst_s = [sb(f"dst_s{k}", [P, 1], U32) for k in range(RING)]
        XG = sb("XG", [P, RING, D])
        XT = sb("XT", [P, RING, P])
        WB = sb("WB", [P, RING, RECORD])
        HT = sb("HT", [P, 2, CHUNKS, P])
        YG = sb("YG", [P, RING, D])

        XA = sb("XA", [P, TPB, D])
        xt_hi = sb("xt_hi", [P, SEQ], F32R)
        xt_lo = sb("xt_lo", [P, SEQ], F32R)
        QK = sb("QK", [P, 2, SEQ])
        qk_hi = sb("qk_hi", [P, 2, SEQ], F32R)
        qk_lo = sb("qk_lo", [P, 2, SEQ], F32R)
        uv_pre = sb("uv_pre", [P, TPB, 2 * D])
        U = sb("U", [P, TILES, D])
        VP = sb("VP", [P, 2, TPB, D + 32])
        KS = sb("KS", [P, 2, GROUPS, SEQ], F32R)
        QS = sb("QS", [P, GROUPS, SEQ])
        QM = sb("QM", [P, 2, GROUPS, HG, SEQ], F32R)
        AT = sb("AT", [P, GROUPS, SEQ])
        Z = sb("Z", [P, TPB, D])
        YT = sb("YT", [P, TPB, P])
        Yt = sb("Yt", [P, TPB, D])
        zst = sb("zst", [P, TPB, 6])
        zmu = sb("zmu", [P, TPB])
        zrs = sb("zrs", [P, TPB])
        PS = ctx.enter_context(nc.psum_tensor("PS", [P, 8, 512], F32))

        names = """made passed loaded  bias_ps bias_out set_up dve_own
            ln_x xn_ready xn_t_ps xn_t logits_ps tops_diff exp_top chosen_made counts_ps
            load_made map_ps src_staged xg_t_ps xt_ready w_staged up_ps gelu_out down_ps y_ready y_loaded
            dst_staged x_out xa_ready xt_ps xt_split qk_ps qk_act uv_ps uv_biased uv_act qk_split rep_ps rep_out qm_ready
            s_ps s_act av_ps at_out z_ps z_gated z_norm yt_ps yt_out y_ps y_out stored""".split()
        S = {n: sem(n) for n in names}
        stored_xn = [sem(f"stored_xn{k}") for k in range(RING)]
        gathered = [sem(f"gathered{k}") for k in range(RING)]
        scattered = [sem(f"scattered{k}") for k in range(RING)]
        y_back = [sem(f"y_back{k}") for k in range(4)]
        w_loads = [sem(f"w_loads{k}") for k in range(2)]
        x_in = [sem(f"x_in{k}") for k in range(4)]
        made, loaded, bias_ps, bias_out, set_up = (
            S[n] for n in ("made", "loaded", "bias_ps", "bias_out", "set_up"))

        MADE = 15
        x_t = x.rearrange("(t p) d -> p t d", p=P)
        out_t = out.rearrange("(t p) d -> p t d", p=P)
        R_B2, R_RB, R_UV, R_YB = 0, EXPERTS * D, EXPERTS * D + EXPERTS, EXPERTS * D + EXPERTS + 2 * D
        OWN_PER_PAIR = 2 * 27
        QTR = TILES // 4

        block = ctx.enter_context(nc.Block())

        @block.sync
        def _(sp):
            for k in range(4):
                sp.dma_start(X[:, k * QTR:(k + 1) * QTR, :], x_t[:, k * QTR:(k + 1) * QTR, :]).then_inc(x_in[k], 16)
            sp.dma_start(rw[:], router_w).then_inc(loaded, 16)
            sp.dma_start(row[:, R_B2:R_RB], fb2.rearrange("(a e) d -> a (e d)", a=1)).then_inc(loaded, 16)
            sp.dma_start(row[:, R_RB:R_UV], router_b.rearrange("(a e) -> a e", a=1)).then_inc(loaded, 16)
            sp.dma_start(row[:, R_UV:R_YB], b1[0:2 * D].rearrange("(a e) -> a e", a=1)).then_inc(loaded, 16)
            sp.dma_start(row[:, R_YB:R_YB + D], b2.rearrange("(a e) -> a e", a=1)).then_inc(loaded, 16)
            sp.dma_start(records[:, :, C_B1:C_B2], fb1.rearrange("e (p c) -> p e c", p=P)).then_inc(loaded, 16)
            sp.dma_start(w_in[:], W1).then_inc(loaded, 16)
            sp.dma_start(w_out[:], W2).then_inc(loaded, 16)
            sp.dma_start(cols[:, 0:1], gamma.rearrange("(p a) -> p a", a=1)).then_inc(loaded, 16)
            sp.dma_start(cols[:, 1:2], beta.rearrange("(p a) -> p a", a=1)).then_inc(loaded, 16)
            for c in (2, 3):
                sp.dma_start(cols[:, 2 + c:3 + c],
                             b1[c * D:(c + 1) * D].rearrange("(p a) -> p a", a=1)).then_inc(loaded, 16)
            sp.dma_start(records[:, :, C_W1:C_W2], w1.rearrange("e d f -> d e f")).then_inc(w_loads[0], 16)
            sp.dma_start(records[:, :, C_W2:C_B1], w2.rearrange("e (p c) d -> p e (c d)", p=P)).then_inc(w_loads[1], 16)

            def ffn(f):
                with sp.Fori(0, TILES // RING) as i:
                    for k in range(RING):
                        t = i * RING + k
                        sp.wait_ge(S["xn_ready"], t + (f * TILES + 1))
                        sp.dma_start(xn_rows[bass.ds(t * P, P), :], XNs[:, k, :]).then_inc(stored_xn[k], 16)
                for k in range(RING):
                    sp.wait_ge(scattered[k], 16 * (f + 1) * SLOT_TILES // RING)
                for c in range(4):
                    rows = y_rows[c * QTR * P * TOPK:(c + 1) * QTR * P * TOPK, :]
                    sp.dma_start(YL[:, c * QTR:(c + 1) * QTR, :, :],
                                 rows.rearrange("(t p j) d -> p t j d", p=P, j=TOPK)).then_inc(y_back[c], 16)

            ffn(0)
            ffn(1)
            for c in range(4):
                sp.wait_ge(S["x_out"], TILES + (c + 1) * QTR)
                sp.dma_start(out_t[:, c * QTR:(c + 1) * QTR, :], X[:, c * QTR:(c + 1) * QTR, :]).then_inc(S["stored"], 16)
            sp.wait_ge(S["stored"], 64)

        @block.gpsimd
        def _(pool):
            def make(ins):
                ins.then_inc(made, 1)

            make(pool.memset(ident[:], 0.0))
            make(pool.memset(before[:], 1.0))
            make(pool.memset(ones[:], 1.0))
            make(pool.memset(ones_h[:], 1.0))
            make(pool.memset(quarter[:], 1.0))
            make(pool.memset(ones8[:], 1.0))
            make(pool.iota(iota[:], pattern=[[1, P]], base=0, channel_multiplier=0,
                           allow_small_or_imprecise_dtypes=True))
            make(pool.iota(token_id[:], pattern=[[P, TILES]], base=0, channel_multiplier=1,
                           allow_small_or_imprecise_dtypes=True))
            make(pool.iota(rank_of[:], pattern=[[-1, EXPERTS]], base=EXPERTS, channel_multiplier=0,
                           allow_small_or_imprecise_dtypes=True))
            make(pool.iota(spare_row[:], pattern=[[P, SLOT_TILES]], base=TOPK * TOKENS + 1, channel_multiplier=1,
                           allow_small_or_imprecise_dtypes=True))
            pool.wait_ge(made, 10)
            make(pool.affine_select(out=ident[:], in_=ident[:], compare_op=ALU.not_equal, fill=1.0, base=0,
                                    pattern=[[-1, P]], channel_multiplier=1))
            make(pool.affine_select(out=before[:], in_=before[:], compare_op=ALU.is_gt, fill=0.0, base=0,
                                    pattern=[[1, P]], channel_multiplier=-1))
            make(pool.memset(VP[:, :, :, D:D + 32], 0.0))
            make(pool.affine_select(out=quarter[:], in_=quarter[:], compare_op=ALU.is_ge, fill=0.0, base=0,
                                    pattern=[[-32, HG]], channel_multiplier=1))
            pool.wait_ge(made, MADE - 1)
            make(pool.affine_select(out=quarter[:], in_=quarter[:], compare_op=ALU.is_ge, fill=0.0, base=31,
                                    pattern=[[32, HG]], channel_multiplier=-1))

            def ffn(f):
                n0, r0 = f * SLOT_TILES, f * (SLOT_TILES // RING)

                def gather(s, k):
                    pool.wait_ge(S["src_staged"], s + (n0 + 1))
                    pool.sem_inc(S["passed"], 1)
                    pool.indirect_dma_start(XG[:, k, :], None, xn_rows,
                                            bass.IndirectOffsetOnAxis(ap=src_s[k][:], axis=0)).then_inc(gathered[k], 16)

                def scatter(s, k):
                    pool.wait_ge(S["y_ready"], s + (n0 + 1))
                    pool.sem_inc(S["passed"], 1)
                    pool.indirect_dma_start(y_rows, bass.IndirectOffsetOnAxis(ap=dst_s[k][:], axis=0),
                                            YG[:, k, :], None).then_inc(scattered[k], 16)

                def group(g, is_last=False, before_last=False):
                    for k in range(RING):
                        if not is_last and not (before_last and k + AHEAD >= 2 * RING):
                            gather(g * RING + k + AHEAD, (k + AHEAD) % RING)
                        scatter(g * RING + k, k)

                for k in range(RING):
                    pool.wait_ge(stored_xn[k], 16 * (f + 1) * TILES // RING)
                for s in range(AHEAD):
                    gather(s, s % RING)
                group(0)
                with pool.Fori(1, SLOT_TILES // RING - 2) as g:
                    group(g)
                group(SLOT_TILES // RING - 2, before_last=True)
                group(SLOT_TILES // RING - 1, is_last=True)

            def masks(b, par):
                for r in range(2):
                    pool.wait_ge(S["rep_out"], b * 4 + (r + 1))
                    if r == 0:
                        wait(pool, S["s_ps"], (b - 1) * 8)
                    pool.sem_inc(S["passed"], 1)
                    for j in range(HG):
                        last = pool.tensor_scalar(QM[:, par, 2 * r:2 * r + 2, j, :], QS[:, 2 * r:2 * r + 2, :],
                                                  quarter[:, j:j + 1], 1.0, ALU.mult, ALU.mult)
                    last.then_inc(S["qm_ready"], 1)

            ffn(0)
            masks(0, 0)
            masks(1, 1)
            with pool.Fori(1, BATCH // 2) as i:
                masks(i * 2, 0)
                masks(i * 2 + 1, 1)
            ffn(1)

        @block.tensor
        def _(pe):
            pe.wait_ge(made, MADE)
            pe.wait_ge(loaded, 16 * 12)
            for h in range(2):
                pe.matmul(PS[:, h, :], ones[0:1, :], row[:, 512 * h:512 * h + 512], start=True, stop=True)
            pe.matmul(PS[:, 2, 0:EXPERTS + 2 * D], ones[0:1, :], row[:, R_RB:R_YB], start=True, stop=True)
            pe.wait_ge(set_up, 1)
            pe.matmul(PS[:, 4, 0:D], beta_all[:], w_out[:], start=True, stop=False)
            pe.matmul(PS[:, 4, 0:D], ones[0:1, :], row[:, R_YB:R_YB + D], start=False, stop=True).then_inc(bias_ps, 1)

            def ffn(f):
                t0, n0 = f * TILES, f * SLOT_TILES
                pe.wait_ge(bias_out, 5)
                with pe.Fori(0, TILES // RING) as i:
                    for k in range(RING):
                        t = i * RING + k
                        pe.wait_ge(S["xn_ready"], t + (t0 + 1))
                        pe.transpose(PS[:, k % 2, 0:P], XNs[:, k, :], ident[:]).then_inc(S["xn_t_ps"], 1)
                        pe.wait_ge(S["xn_t"], t + (t0 + 1))
                        pe.matmul(PS[:, 4, bass.ds(t * EXPERTS, EXPERTS)], XTr[:, k % 2, :], rw[:],
                                  start=True, stop=True).then_inc(S["logits_ps"], 1)
                pe.wait_ge(S["chosen_made"], f + 1)
                every = chosen[:].rearrange("p t e -> p (t e)")
                pe.matmul(PS[:, 6, 0:P], before[:], every, start=True, stop=True)
                pe.matmul(PS[:, 7, 0:P], ones_h[:], every, start=True, stop=True).then_inc(S["counts_ps"], 1)
                pe.wait_ge(S["load_made"], f + 1)
                for n in range(TOPK * TILES):
                    mm = pe.matmul(PS[:, 5, 0:2 * SLOT_TILES], in_tile[:, n, :],
                                   tile_load[:, n, :, :].rearrange("p a s -> p (a s)"),
                                   start=(n == 0), stop=(n == TOPK * TILES - 1))
                mm.then_inc(S["map_ps"], 1)

                def turn(s, k, g):
                    pe.wait_ge(gathered[k], (g + (f * SLOT_TILES // RING + 1)) * 16)
                    wait(pe, S["xt_ready"], s + (n0 - 1))
                    pe.transpose(PS[:, k % 2, 0:P], XG[:, k, :], ident[:]).then_inc(S["xg_t_ps"], 1)

                def up(s, k):
                    pe.wait_ge(S["xt_ready"], s + (n0 + 1))
                    pe.wait_ge(S["w_staged"], s + (n0 + 1))
                    wait(pe, S["gelu_out"], (s + (n0 - 1)) * CHUNKS)
                    for c in range(CHUNKS):
                        mm = pe.matmul(PS[:, 2 + k % 2, c * P:(c + 1) * P], WB[:, k, C_W1 + c:C_W1 + FF:CHUNKS],
                                       XT[:, k, :], start=True, stop=True)
                    mm.then_inc(S["up_ps"], 1)

                def down(s, k):
                    wait(pe, S["y_ready"], s + (n0 - 1))
                    for c in range(CHUNKS):
                        pe.wait_ge(S["gelu_out"], (s + n0) * CHUNKS + (c + 1))
                        mm = pe.matmul(PS[:, 4 + k % 2, 0:D], HT[:, k % 2, c, :],
                                       WB[:, k, C_W2 + c * D:C_W2 + (c + 1) * D],
                                       start=(c == 0), stop=(c == CHUNKS - 1))
                    mm.then_inc(S["down_ps"], 1)

                def group(g, is_last):
                    for k in range(RING):
                        if not (is_last and k + 2 >= RING):
                            turn(g * RING + k + 2, (k + 2) % RING, g + (k + 2) // RING)
                        if not (is_last and k + 1 >= RING):
                            up(g * RING + k + 1, (k + 1) % RING)
                        down(g * RING + k, k)

                turn(0, 0, 0)
                turn(1, 1, 0)
                up(0, 0)
                group(0, False)
                with pe.Fori(1, SLOT_TILES // RING - 1) as g:
                    group(g, False)
                group(SLOT_TILES // RING - 1, True)

            def project(b, part):
                if part == "turn":
                    pe.wait_ge(S["xa_ready"], b + 1)
                    if isinstance(b, int) and b < 3:
                        wait(pe, S["rep_out"], 4 * (b - 1) + 3)
                    else:
                        pe.wait_ge(S["z_gated"], b * 2 - 5)
                    for t in range(TPB):
                        mm = pe.transpose(PS[:, 5, t * P:(t + 1) * P], XA[:, t, :], ident[:])
                    mm.then_inc(S["xt_ps"], 1)
                elif part == "qk":
                    pe.wait_ge(S["xt_split"], b + 1)
                    if isinstance(b, int) and b < 3:
                        wait(pe, S["rep_out"], 4 * b)
                    else:
                        pe.wait_ge(S["z_gated"], b * 2 - 4)
                    for c in range(2):
                        q = slice((2 + c) * D, (3 + c) * D)
                        for n, (w, m) in enumerate(((w_in_hi, xt_hi), (w_in_hi, xt_lo), (w_in_lo, xt_hi))):
                            mm = pe.matmul(PS[:, 4, c * SEQ:(c + 1) * SEQ], w[:, q], m[:], start=(n == 0), stop=(n == 2))
                    mm.then_inc(S["qk_ps"], 1)
                else:
                    pe.wait_ge(S["rep_out"], b * 4 + 1)
                    for t in range(TPB):
                        q = slice(t * P, (t + 1) * P)
                        for n, (m, w) in enumerate(((xt_hi, w_in_hi), (xt_lo, w_in_hi), (xt_hi, w_in_lo))):
                            mm = pe.matmul(PS[:, 4, t * 2 * D:(t + 1) * 2 * D], m[:, q], w[:, 0:2 * D],
                                           start=(n == 0), stop=(n == 2))
                    mm.then_inc(S["uv_ps"], 1)

            def replicate(b, r):
                c, bank = r // 2, (4, 5, 5, 4)[r]
                if r == 0:
                    pe.wait_ge(S["qk_split"], b + 1)
                    wait(pe, S["y_out"], b - 2)
                elif r == 1:
                    wait(pe, S["yt_out"], b - 2)
                elif r == 2:
                    pe.wait_ge(S["rep_out"], b * 4 + 2)
                else:
                    pe.wait_ge(S["uv_biased"], b + 1)
                for h in range(2):
                    g = 2 * (r % 2) + h
                    pe.matmul(PS[:, bank, h * SEQ:(h + 1) * SEQ], spread[:, 2 * c, g, :], qk_hi[:, c, :],
                              start=True, stop=False)
                    mm = pe.matmul(PS[:, bank, h * SEQ:(h + 1) * SEQ], spread[:, 2 * c + 1, g, :], qk_lo[:, c, :],
                                   start=False, stop=True)
                mm.then_inc(S["rep_ps"], 1)

            def scores(b, par, n):
                g, kt = n // 2, n % 2
                if n % 4 == 0:
                    pe.wait_ge(S["qm_ready"], b * 2 + (n // 4 + 1))
                    pe.wait_ge(S["rep_out"], b * 4 + (n // 4 + 3))
                wait(pe, S["s_act"], b * 8 + (n - 1))
                for h in range(2):
                    mm = pe.matmul(PS[:, 2 * (n % 2) + h, :], KS[:, par, g, kt * P:(kt + 1) * P],
                                   QM[:, par, g, 2 * h:2 * h + 2, :].rearrange("p j q -> p (j q)"),
                                   start=True, stop=True)
                mm.then_inc(S["s_ps"], 1)

            def attend(b, par, g):
                pe.wait_ge(S["uv_act"], b + 1)
                if g % 2 == 0:
                    wait(pe, S["at_out"], b * 2 + (g // 2 - 1))
                pe.wait_ge(S["s_act"], b * 8 + (2 * g + 2))
                for kt in range(TPB):
                    for j in range(HG):
                        h = (HG * g + j) * HD
                        mm = pe.matmul(PS[32 * j:32 * j + 32, 6 + g // 2, (g % 2) * SEQ:(g % 2 + 1) * SEQ],
                                       VP[:, par, kt, h:h + 32], A[:, (2 * g + kt) % 4, j, :],
                                       start=(kt == 0), stop=(kt == TPB - 1), tile_position=(0, 32 * j))
                mm.then_inc(S["av_ps"], 1)

            def back(b, t):
                if t == 0:
                    pe.wait_ge(S["at_out"], b * 2 + 2)
                if isinstance(b, int) and b >= BATCH - 2:
                    pe.wait_ge(S["y_out" if t else "yt_out"], b)
                else:
                    pe.wait_ge(S["rep_out"], b * 4 + (11 + t))
                for g in range(GROUPS):
                    mm = pe.transpose(PS[:, 5 - t, g * P:(g + 1) * P], AT[:, g, t * P:(t + 1) * P], ident[:])
                mm.then_inc(S["z_ps"], 1)

            def output(b, part):
                if part == "turn":
                    pe.wait_ge(S["z_norm"], b + 1)
                    if not isinstance(b, int) or b < BATCH - 3:
                        pe.wait_ge(S["xt_split"], b + 4)
                    for t in range(TPB):
                        mm = pe.transpose(PS[:, 5, t * P:(t + 1) * P], Z[:, t, :], ident[:])
                    mm.then_inc(S["yt_ps"], 1)
                else:
                    pe.wait_ge(S["yt_out"], b + 1)
                    if not isinstance(b, int) or b < BATCH - 3:
                        pe.wait_ge(S["qk_act"], b + 4)
                    for t in range(TPB):
                        mm = pe.matmul(PS[:, 4, t * D:(t + 1) * D], YT[:, t, :], w_out_g[:], start=True, stop=True)
                    mm.then_inc(S["y_ps"], 1)

            def step(b, par, older=True, newer=2):
                scores(b, par, 0)
                scores(b, par, 1)
                if older:
                    attend(b - 1, 1 - par, 3)
                if newer:
                    replicate(b + 1, 0)
                    replicate(b + 1, 1)
                scores(b, par, 2)
                attend(b, par, 0)
                if newer:
                    project(b + 1, "uv")
                scores(b, par, 3)
                if newer:
                    replicate(b + 1, 2)
                    replicate(b + 1, 3)
                scores(b, par, 4)
                attend(b, par, 1)
                if older:
                    back(b - 1, 0)
                scores(b, par, 5)
                if older:
                    back(b - 1, 1)
                if newer > 1:
                    project(b + 2, "turn")
                scores(b, par, 6)
                attend(b, par, 2)
                if newer > 1:
                    project(b + 2, "qk")
                scores(b, par, 7)
                if older:
                    output(b - 1, "turn")
                    output(b - 1, "out")

            def attention():
                pe.wait_ge(S["y_ready"], SLOT_TILES)
                pe.wait_ge(S["gelu_out"], SLOT_TILES * CHUNKS)
                pe.wait_ge(set_up, 3)
                project(0, "turn")
                project(0, "qk")
                replicate(0, 0)
                replicate(0, 1)
                project(0, "uv")
                replicate(0, 2)
                replicate(0, 3)
                project(1, "turn")
                project(1, "qk")
                step(0, 0, older=False)
                step(1, 1)
                with pe.Fori(1, BATCH // 2 - 1) as i:
                    step(i * 2, 0)
                    step(i * 2 + 1, 1)
                step(BATCH - 2, 0, newer=1)
                step(BATCH - 1, 1, newer=0)
                b = BATCH - 1
                attend(b, 1, 3)
                back(b, 0)
                back(b, 1)
                output(b, "turn")
                output(b, "out")

            ffn(0)
            attention()
            ffn(1)

        @block.scalar
        def _(act):
            def ffn(f):
                t0, n0 = f * TILES, f * SLOT_TILES
                with act.Fori(0, TILES // RING) as i:
                    for k in range(RING):
                        t = i * RING + k
                        act.wait_ge(S["xn_t_ps"], t + (t0 + 1))
                        act.copy(XTr[:, k % 2, :], PS[:, k % 2, 0:P]).then_inc(S["xn_t"], 1)
                act.wait_ge(S["tops_diff"], f + 1)
                act.activation(scr[1][:], scr[0][:], ACT.Exp).then_inc(S["exp_top"], 1)

                def gelu(s, k):
                    wait(act, S["down_ps"], s + (n0 - 1))
                    act.wait_ge(S["up_ps"], s + (n0 + 1))
                    for c in range(CHUNKS):
                        act.activation(HT[:, k % 2, c, :], PS[:, 2 + k % 2, c * P:(c + 1) * P], ACT.Gelu,
                                       bias=WB[:, k, C_B1 + c:C_B1 + c + 1]).then_inc(S["gelu_out"], 1)

                for k in range(RING):
                    gelu(k, k)
                with act.Fori(1, SLOT_TILES // RING) as g:
                    for k in range(RING):
                        gelu(g * RING + k, k)

            def silu_scores(b, n):
                act.wait_ge(S["s_ps"], b * 8 + (n + 1))
                if n % 2 == 0:
                    wait(act, S["av_ps"], b * 4 + (n // 2 - 1))
                act.activation(A[:, n % 4, :, :].rearrange("p j q -> p (j q)"),
                               PS[:, 2 * (n % 2):2 * (n % 2) + 2, :].rearrange("p a q -> p (a q)"),
                               ACT.Silu).then_inc(S["s_act"], 1)

            def silu_qk(b):
                act.wait_ge(S["qk_ps"], b + 1)
                wait(act, S["qk_split"], b)
                for c in range(2):
                    a = act.activation(QK[:, c, :], PS[:, 4, c * SEQ:(c + 1) * SEQ], ACT.Silu, bias=cols[:, 4 + c:5 + c])
                a.then_inc(S["qk_act"], 1)

            def silu_uv(b, par):
                act.wait_ge(S["uv_biased"], b + 1)
                wait(act, S["av_ps"], (b - 1) * 4)
                act.activation(U[:, bass.ds(b * TPB, TPB), :], uv_pre[:, :, 0:D], ACT.Silu)
                act.activation(VP[:, par, :, 0:D], uv_pre[:, :, D:2 * D], ACT.Silu).then_inc(S["uv_act"], 1)

            def step(b, par, newer=2):
                for n in range(4):
                    silu_scores(b, n)
                if newer:
                    silu_uv(b + 1, 1 - par)
                for n in range(4, 7):
                    silu_scores(b, n)
                if newer > 1:
                    silu_qk(b + 2)
                silu_scores(b, 7)

            ffn(0)
            silu_qk(0)
            silu_uv(0, 0)
            silu_qk(1)
            step(0, 0)
            step(1, 1)
            with act.Fori(1, BATCH // 2 - 1) as i:
                step(i * 2, 0)
                step(i * 2 + 1, 1)
            step(BATCH - 2, 0, newer=1)
            step(BATCH - 1, 1, newer=0)
            ffn(1)

        @block.vector
        def _(dve):
            own = Steps(dve, S["dve_own"])
            link = own.done

            def ln_coefficients(st, mu, rs, w):
                link(dve.tensor_tensor(w[0], st[:, :, 1], st[:, :, 4], ALU.subtract))
                dve.tensor_tensor(w[1], st[:, :, 2], st[:, :, 5], ALU.add).then_inc(S["dve_own"], 1)
                own.count += 1
                link(dve.tensor_tensor(mu, st[:, :, 1], st[:, :, 4], ALU.add))
                link(dve.scalar_tensor_tensor(out=w[0], in0=w[0], scalar=0.25, in1=w[0], op0=ALU.mult, op1=ALU.mult))
                link(dve.scalar_tensor_tensor(out=w[1], in0=w[1], scalar=1.0 / D, in1=w[0], op0=ALU.mult, op1=ALU.add))
                link(dve.tensor_scalar(mu, mu, 0.5, None, ALU.mult))
                link(dve.tensor_scalar(w[1], w[1], EPS, None, ALU.add))
                link(dve.tensor_scalar(w[2].bitcast(I32), w[1].bitcast(I32), 1, None, ALU.logical_shift_right))
                link(dve.tensor_scalar(rs.bitcast(I32), w[2].bitcast(I32), -1.0, float(RSQRT_SEED), ALU.mult, ALU.add))
                link(dve.tensor_scalar(w[1], w[1], -0.5, None, ALU.mult))
                for _ in range(4):
                    link(dve.tensor_tensor(w[2], rs, rs, ALU.mult))
                    link(dve.tensor_tensor(w[2], w[2], w[1], ALU.mult))
                    link(dve.scalar_tensor_tensor(out=rs, in0=w[2], scalar=1.5, in1=rs, op0=ALU.add, op1=ALU.mult))

            def layernorm_stats(f_first):
                if f_first:
                    for c in range(4):
                        dve.wait_ge(x_in[c], 16)
                with dve.Fori(0, TILES // RING) as i:
                    own.enter(i, RING)
                    for k in range(RING):
                        dve.bn_stats(stats[:, bass.ds(i * RING + k, 1), :].rearrange("p a s -> p (a s)"),
                                     X[:, bass.ds(i * RING + k, 1), :].rearrange("p a d -> p (a d)")
                                     ).then_inc(S["dve_own"], 1)
                        own.count += 1
                    dve.wait_ge(S["dve_own"], own.turn + own.count)
                own.leave(TILES // RING)
                ln_coefficients(stats[:], mean[:], rstd[:], [w[:] for w in scr])

            def normalize(dst, t):
                src = X[:, bass.ds(t, 1), :].rearrange("p a d -> p (a d)")
                return dve.tensor_scalar(dst, src, mean[:, bass.ds(t, 1)], rstd[:, bass.ds(t, 1)],
                                         ALU.subtract, ALU.mult)

            def ffn(f):
                t0, n0 = f * TILES, f * SLOT_TILES
                layernorm_stats(f == 0)

                def rows(i):
                    for k in range(RING):
                        wait(dve, S["xn_t_ps"], i * RING + (k + t0 - 3))
                        wait(dve, stored_xn[k], (i + f * (TILES // RING)) * 16)
                        normalize(XNs[:, k, :], i * RING + k).then_inc(S["xn_ready"], 1)

                rows(0)
                with dve.Fori(1, TILES // RING) as i:
                    rows(i)
                dve.wait_ge(S["logits_ps"], t0 + TILES)
                link(dve.tensor_tensor(LG[:], PS[:, 4, 0:TILES * EXPERTS].rearrange("p (t e) -> p t e", e=EXPERTS),
                                       rb_all[:].unsqueeze(1).to_broadcast([P, TILES, EXPERTS]), ALU.add))
                ranks = rank_of[:].unsqueeze(1).to_broadcast([P, TILES, EXPERTS])
                for j in range(TOPK):
                    link(dve.tensor_reduce(top[:, j, :], LG[:], AX.X, ALU.max))
                    link(dve.tensor_tensor(weighed[:], LG[:],
                                           top[:, j, :].unsqueeze(2).to_broadcast([P, TILES, EXPERTS]), ALU.is_equal))
                    link(dve.tensor_tensor(weighed[:], weighed[:], ranks, ALU.mult))
                    link(dve.tensor_reduce(first[:], weighed[:], AX.X, ALU.max))
                    link(dve.tensor_tensor(one_hot[:, j, :, :], ranks,
                                           first[:].unsqueeze(2).to_broadcast([P, TILES, EXPERTS]), ALU.is_equal))
                    if j == 0:
                        link(dve.scalar_tensor_tensor(out=LG[:], in0=one_hot[:, 0, :, :], scalar=-3.0e38, in1=LG[:],
                                                      op0=ALU.mult, op1=ALU.add))
                dve.tensor_tensor(scr[0][:], top[:, 1, :], top[:, 0, :], ALU.subtract).then_inc(S["tops_diff"], 1)
                dve.tensor_tensor(chosen[:], one_hot[:, 0, :, :], one_hot[:, 1, :, :], ALU.add).then_inc(S["chosen_made"], 1)
                dve.wait_ge(S["exp_top"], f + 1)
                link(dve.tensor_scalar(scr[2][:], scr[1][:], 1.0, None, ALU.add))
                link(dve.reciprocal(scr[3][:], scr[2][:]))
                link(dve.tensor_scalar(half_gate[:, 0, :], scr[3][:], 0.5, None, ALU.mult))
                link(dve.tensor_tensor(half_gate[:, 1, :], half_gate[:, 0, :], scr[1][:], ALU.mult))
                totals = PS[:, 7, 0:P].rearrange("p (t e) -> p t e", e=EXPERTS)
                ahead = PS[:, 6, 0:P].rearrange("p (t e) -> p t e", e=EXPERTS)
                dve.wait_ge(S["counts_ps"], f + 1)
                link(dve.tensor_copy(run[0][:], totals))
                a, reach = 0, 1
                while reach < TILES:
                    link(dve.tensor_copy(run[1 - a][:, 0:reach, :], run[a][:, 0:reach, :]))
                    link(dve.tensor_tensor(run[1 - a][:, reach:, :], run[a][:, reach:, :],
                                           run[a][:, 0:TILES - reach, :], ALU.add))
                    a, reach = 1 - a, 2 * reach
                upto = run[a]
                link(dve.tensor_scalar(n_int[:], upto[:, TILES - 1, :], float(P - 1), None, ALU.add))
                link(dve.tensor_scalar(n_int[:], n_int[:], 7, None, ALU.logical_shift_right))
                link(dve.tensor_copy(n_tiles[:], n_int[:]))
                link(dve.tensor_tensor_scan(n_upto[:], ones8[:], n_tiles[:], 0.0, ALU.mult, ALU.add))
                link(dve.tensor_tensor(base[:], n_upto[:], n_tiles[:], ALU.subtract))
                link(dve.tensor_scalar(base[:], base[:], float(P), None, ALU.mult))
                link(dve.tensor_tensor(te_cmp[:], iota[0:1, 0:SLOT_TILES].unsqueeze(2).to_broadcast([1, SLOT_TILES, EXPERTS]),
                                       n_upto[0:1, :].unsqueeze(1).to_broadcast([1, SLOT_TILES, EXPERTS]), ALU.is_ge))
                link(dve.tensor_reduce(te_sum[:], te_cmp[:], AX.X, ALU.add))
                link(dve.tensor_scalar(tile_expert[:], te_sum[:], float(EXPERTS - 1), None, ALU.min))
                link(dve.tensor_tensor(place[:], upto[:], totals, ALU.subtract))
                link(dve.tensor_tensor(place[:], place[:], ahead, ALU.add))
                link(dve.tensor_tensor(place[:], place[:], base[:].unsqueeze(1).to_broadcast([P, TILES, EXPERTS]), ALU.add))
                for j in range(TOPK):
                    link(dve.tensor_tensor(weighed[:], place[:], one_hot[:, j, :, :], ALU.mult))
                    link(dve.tensor_reduce(slot_f[:, j * TILES:(j + 1) * TILES], weighed[:], AX.X, ALU.add))
                link(dve.tensor_copy(slot_i[:], slot_f[:]))
                link(dve.tensor_scalar(slot_lo_i[:], slot_i[:], P - 1, None, ALU.bitwise_and))
                link(dve.tensor_scalar(slot_hi_i[:], slot_i[:], 7, None, ALU.logical_shift_right))
                link(dve.tensor_copy(slot_lo[:], slot_lo_i[:]))
                link(dve.tensor_copy(slot_hi[:], slot_hi_i[:]))
                N = TOPK * TILES
                link(dve.tensor_tensor(tile_hot, iota[:, 0:SLOT_TILES].unsqueeze(1).to_broadcast([P, N, SLOT_TILES]),
                                       slot_hi[:].unsqueeze(2).to_broadcast([P, N, SLOT_TILES]), ALU.is_equal))
                for j in range(TOPK):
                    q = slice(j * TILES, (j + 1) * TILES)
                    link(dve.tensor_tensor(tile_load[:, q, 0, :], tile_hot[:, q, :],
                                           token_id[:].unsqueeze(2).to_broadcast([P, TILES, SLOT_TILES]), ALU.mult))
                    link(dve.tensor_scalar(tile_load[:, q, 1, :], tile_hot[:, q, :], float(j + 1), None, ALU.mult))
                dve.tensor_tensor(in_tile, iota[:].unsqueeze(1).to_broadcast([P, N, P]),
                                  slot_lo[:].unsqueeze(2).to_broadcast([P, N, P]), ALU.is_equal).then_inc(S["load_made"], 1)
                dve.wait_ge(S["map_ps"], f + 1)
                link(dve.tensor_copy(slot_map[:], PS[:, 5, 0:2 * SLOT_TILES].rearrange("p (a s) -> p a s", a=2)))
                link(dve.tensor_copy(src_row[:], slot_map[:, 0, :]))
                link(dve.tensor_scalar(dst_f[:], slot_map[:, 1, :], 0.0, None, ALU.is_equal))
                link(dve.tensor_tensor(dst_f[:], dst_f[:], spare_row[:], ALU.mult))
                link(dve.scalar_tensor_tensor(out=dst_f[:], in0=dst_f[:], scalar=-1.0, in1=slot_map[:, 1, :],
                                              op0=ALU.add, op1=ALU.add))
                link(dve.scalar_tensor_tensor(out=dst_row[:], in0=slot_map[:, 0, :], scalar=float(TOPK), in1=dst_f[:],
                                              op0=ALU.mult, op1=ALU.add))

                def stage_src(s, k):
                    wait(dve, S["xg_t_ps"], s + (n0 - 3))
                    dve.tensor_copy(src_s[k][:], src_row[:, bass.ds(s, 1)]).then_inc(S["src_staged"], 1)

                def stage_weights(s, k):
                    wait(dve, S["y_ready"], s + (n0 - 3))
                    e = dve.value_load(tile_expert[0:1, bass.ds(s, 1)], min_val=0, max_val=EXPERTS - 1)
                    dve.tensor_copy(WB[:, k, :], records[:, bass.ds(e, 1), :].rearrange("p a r -> p (a r)")
                                    ).then_inc(S["w_staged"], 1)

                def evacuate_x(s, k):
                    dve.wait_ge(S["xg_t_ps"], s + (n0 + 1))
                    wait(dve, S["up_ps"], s + (n0 - 3))
                    dve.tensor_copy(XT[:, k, :], PS[:, k % 2, 0:P]).then_inc(S["xt_ready"], 1)

                def evacuate_y(s, k, g):
                    wait(dve, scattered[k], (g + f * (SLOT_TILES // RING)) * 16)
                    dve.tensor_copy(dst_s[k][:], dst_row[:, bass.ds(s, 1)]).then_inc(S["dst_staged"], 1)
                    dve.wait_ge(S["down_ps"], s + (n0 + 1))
                    dve.wait_ge(S["w_staged"], s + (n0 + 1))
                    dve.tensor_tensor(YG[:, k, :], PS[:, 4 + k % 2, 0:D], WB[:, k, C_B2:RECORD], ALU.add
                                      ).then_inc(S["y_ready"], 1)

                def group(g, is_last=False, before_last=False):
                    for k in range(RING):
                        if not is_last and not (before_last and k + AHEAD >= 2 * RING):
                            stage_src(g * RING + k + AHEAD, (k + AHEAD) % RING)
                        if not (is_last and k + 2 >= RING):
                            stage_weights(g * RING + k + 2, (k + 2) % RING)
                            evacuate_x(g * RING + k + 2, (k + 2) % RING)
                        evacuate_y(g * RING + k, k, g)

                for s in range(RING):
                    stage_src(s, s)
                if f == 0:
                    for q in w_loads:
                        dve.wait_ge(q, 16)
                for s in range(2):
                    stage_weights(s, s)
                    evacuate_x(s, s)
                    if s + RING < AHEAD:
                        stage_src(s + RING, s)
                group(0)
                with dve.Fori(1, SLOT_TILES // RING - 2) as g:
                    group(g)
                group(SLOT_TILES // RING - 2, before_last=True)
                group(SLOT_TILES // RING - 1, is_last=True)
                for c in range(4):
                    dve.wait_ge(y_back[c], (f + 1) * 16)
                turns = TILES // RING
                with dve.Fori(0, turns) as i:
                    own.enter(i, RING)
                    for j in range(TOPK):
                        for k in range(RING):
                            t = i * RING + k
                            xt = X[:, bass.ds(t, 1), :].rearrange("p a d -> p (a d)")
                            yt = YL[:, bass.ds(t, 1), j, :].rearrange("p a d -> p (a d)")
                            ins = dve.scalar_tensor_tensor(out=xt, in0=yt, scalar=half_gate[:, j, bass.ds(t, 1)],
                                                           in1=xt, op0=ALU.mult, op1=ALU.add)
                            if j == 0:
                                ins.then_inc(S["dve_own"], 1)
                                own.count += 1
                            else:
                                ins.then_inc(S["x_out"], 1)
                        if j == 0:
                            dve.wait_ge(S["dve_own"], own.turn + own.count)
                own.leave(turns)
                dve.wait_ge(S["x_out"], t0 + TILES)

            def prepare(b):
                wait(dve, S["xt_ps"], b)
                for t in range(TPB):
                    n = normalize(XA[:, t, :], b * TPB + t)
                n.then_inc(S["xa_ready"], 1)

            def split_x(b):
                dve.wait_ge(S["xt_ps"], b + 1)
                wait(dve, S["uv_ps"], b)
                link(dve.tensor_copy(xt_hi[:], PS[:, 5, 0:SEQ]))
                dve.tensor_tensor(xt_lo[:], PS[:, 5, 0:SEQ], xt_hi[:].bitcast(F32), ALU.subtract).then_inc(S["xt_split"], 1)

            def split_qk(b):
                dve.wait_ge(S["qk_act"], b + 1)
                wait(dve, S["rep_ps"], b * 4)
                link(dve.tensor_copy(qk_hi[:], QK[:]))
                dve.tensor_tensor(qk_lo[:], QK[:], qk_hi[:].bitcast(F32), ALU.subtract).then_inc(S["qk_split"], 1)

            def bias_uv(b):
                dve.wait_ge(S["uv_ps"], b + 1)
                wait(dve, S["uv_act"], b)
                dve.tensor_tensor(uv_pre[:], PS[:, 4, :].rearrange("p (t d) -> p t d", t=TPB),
                                  uvb_all[:].unsqueeze(1).to_broadcast([P, TPB, 2 * D]), ALU.add).then_inc(S["uv_biased"], 1)

            def copy_rep(b, par, r):
                dve.wait_ge(S["rep_ps"], b * 4 + (r + 1))
                g, bank = 2 * (r % 2), (4, 5, 5, 4)[r]
                src = PS[:, bank, :].rearrange("p (g q) -> p g q", g=2)
                if r < 2:
                    wait(dve, S["qm_ready"], b * 2 + (r - 1))
                    dve.tensor_copy(QS[:, g:g + 2, :], src).then_inc(S["rep_out"], 1)
                else:
                    wait(dve, S["s_ps"], (b - 1) * 8)
                    dve.tensor_copy(KS[:, par, g:g + 2, :], src).then_inc(S["rep_out"], 1)

            def copy_heads(b, h):
                dve.wait_ge(S["av_ps"], b * 4 + (2 * h + 2))
                wait(dve, S["z_ps"], b * 2)
                dve.tensor_copy(AT[:, 2 * h:2 * h + 2, :], PS[:, 6 + h, :].rearrange("p (g q) -> p g q", g=2)
                                ).then_inc(S["at_out"], 1)

            def gate(b, t):
                dve.wait_ge(S["z_ps"], b * 2 + (t + 1))
                if t == 0:
                    wait(dve, S["yt_ps"], b)
                heads = PS[:, 5 - t, :].rearrange("p (h r) -> p h r", r=32)[:, :, 0:HD]
                u = U[:, bass.ds(b * TPB + t, 1), :].rearrange("p a (h r) -> p (a h) r", r=HD)
                dve.scalar_tensor_tensor(out=Z[:, t, :].rearrange("p (h r) -> p h r", r=HD), in0=heads,
                                         scalar=1.0 / SEQ, in1=u, op0=ALU.mult, op1=ALU.mult).then_inc(S["z_gated"], 1)

            def norm_z(b):
                dve.wait_ge(S["z_gated"], b * 2 + 2)
                for t in range(TPB):
                    dve.bn_stats(zst[:, t, :], Z[:, t, :]).then_inc(S["dve_own"], 1)
                    own.count += 1
                dve.wait_ge(S["dve_own"], own.turn + own.count)
                ln_coefficients(zst[:], zmu[:], zrs[:], [w[:, 0:TPB] for w in scr])
                for t in range(TPB):
                    n = dve.tensor_scalar(Z[:, t, :], Z[:, t, :], zmu[:, t:t + 1], zrs[:, t:t + 1], ALU.subtract, ALU.mult)
                n.then_inc(S["z_norm"], 1)

            def copy_yt(b):
                dve.wait_ge(S["yt_ps"], b + 1)
                wait(dve, S["y_ps"], b)
                dve.tensor_copy(YT[:], PS[:, 5, 0:SEQ].rearrange("p (t d) -> p t d", t=TPB)).then_inc(S["yt_out"], 1)

            def add_y(b):
                dve.wait_ge(S["y_ps"], b + 1)
                link(dve.tensor_tensor(Yt[:], PS[:, 4, 0:TPB * D].rearrange("p (t d) -> p t d", t=TPB),
                                       yb_all[:].unsqueeze(1).to_broadcast([P, TPB, D]), ALU.add))
                x2 = X[:, bass.ds(b * TPB, TPB), :]
                dve.tensor_tensor(x2, x2, Yt[:], ALU.add).then_inc(S["y_out"], 1)

            def step(b, par, older=True, newer=2):
                if older:
                    copy_heads(b - 1, 1)
                if newer > 1:
                    prepare(b + 2)
                if newer:
                    copy_rep(b + 1, 1 - par, 0)
                    copy_rep(b + 1, 1 - par, 1)
                    bias_uv(b + 1)
                    copy_rep(b + 1, 1 - par, 2)
                    copy_rep(b + 1, 1 - par, 3)
                if older:
                    gate(b - 1, 0)
                    gate(b - 1, 1)
                if newer > 1:
                    split_x(b + 2)
                copy_heads(b, 0)
                if older:
                    norm_z(b - 1)
                if newer > 1:
                    split_qk(b + 2)
                if older:
                    copy_yt(b - 1)
                    add_y(b - 1)

            def attention():
                layernorm_stats(False)
                prepare(0)
                split_x(0)
                split_qk(0)
                copy_rep(0, 0, 0)
                copy_rep(0, 0, 1)
                bias_uv(0)
                copy_rep(0, 0, 2)
                copy_rep(0, 0, 3)
                prepare(1)
                split_x(1)
                split_qk(1)
                step(0, 0, older=False)
                step(1, 1)
                with dve.Fori(0, BATCH // 2 - 2) as i:
                    own.enter(i, OWN_PER_PAIR)
                    step(i * 2 + 2, 0)
                    step(i * 2 + 3, 1)
                own.leave(BATCH // 2 - 2)
                step(BATCH - 2, 0, newer=1)
                step(BATCH - 1, 1, newer=0)
                b = BATCH - 1
                copy_heads(b, 1)
                gate(b, 0)
                gate(b, 1)
                norm_z(b)
                copy_yt(b)
                add_y(b)

            dve.wait_ge(loaded, 16 * 12)
            dve.wait_ge(made, MADE)
            dve.tensor_copy(beta_all[:], cols[:, 1:2].to_broadcast([P, P])).then_inc(set_up, 1)
            dve.tensor_scalar(w_out_g[:], w_out[:], cols[:, 0:1], None, ALU.mult).then_inc(set_up, 1)
            link(dve.tensor_copy(w_in_hi[:], w_in[:]))
            link(dve.tensor_tensor(w_in_lo[:], w_in[:], w_in_hi[:].bitcast(F32), ALU.subtract))
            link(dve.memset(spread[:].bitcast(F32), 0.0))
            picks = ident[:].rearrange("p (h d) -> p h d", d=HD)
            for part, copies in enumerate(((0, 1), (2, 3), (0, 2), (1, 3))):
                to = spread[:, part, :, :].rearrange("p g (j r d) -> p (g j) r d", r=REP, d=HD)
                for r in copies:
                    last = dve.tensor_copy(to[:, :, r, :], picks)
            last.then_inc(set_up, 1)
            dve.wait_ge(bias_ps, 1)
            for h in range(2):
                dve.tensor_copy(records[:, 4 * h:4 * h + 4, C_B2:RECORD],
                                PS[:, h, :].rearrange("p (e d) -> p e d", d=D)).then_inc(bias_out, 1)
            dve.tensor_copy(rb_all[:], PS[:, 2, 0:EXPERTS]).then_inc(bias_out, 1)
            dve.tensor_copy(uvb_all[:], PS[:, 2, EXPERTS:EXPERTS + 2 * D]).then_inc(bias_out, 1)
            dve.tensor_copy(yb_all[:], PS[:, 4, 0:D]).then_inc(bias_out, 1)
            dve.wait_ge(bias_out, 5)
            ffn(0)
            attention()
            ffn(1)


INPUTS = ["L0_attn_x", "L0_attn_W1", "L0_attn_b1", "L0_attn_W2", "L0_attn_b2", "L0_attn_gamma", "L0_attn_beta",
          "L0_ffn_router_w", "L0_ffn_router_b", "L0_ffn_w1", "L0_ffn_b1", "L0_ffn_w2", "L0_ffn_b2"]


def kernel(**inputs):
    import concourse.bacc as bacc
    from concourse.bass_utils import run_bass_kernel_spmd

    nc = bacc.Bacc("TRN2", target_bir_lowering=False, num_devices=1)
    arrays, args = {}, []
    for name in INPUTS:
        a = np.ascontiguousarray(inputs[name])
        if name == "L0_attn_x":
            a = a.reshape(TOKENS, D)
        arrays[f"in_{name}"] = a
        args.append(nc.dram_tensor(f"in_{name}", a.shape, mybir.dt.from_np(a.dtype), kind="ExternalInput").ap())
    args.append(nc.dram_tensor("out", (TOKENS, D), F32, kind="ExternalOutput").ap())
    macaron(nc, *args)
    result = run_bass_kernel_spmd(nc, [arrays], core_ids=[0])
    return result.results[0]["out"].reshape(BATCH, SEQ, D)
```

```python
from contextlib import ExitStack

import numpy as np

import concourse.bass as bass
from concourse import mybir

F32 = mybir.dt.float32
F32R = mybir.dt.float32r
F16 = mybir.dt.float16
BF16 = mybir.dt.bfloat16
I32 = mybir.dt.int32
U32 = mybir.dt.uint32
ALU = mybir.AluOpType
ACT = mybir.ActivationFunctionType
AX = mybir.AxisListType

P = 128
D = 128
BATCH, SEQ = 8, 256
TOKENS = BATCH * SEQ
TILES = TOKENS // P
TPB = SEQ // P
HEADS, HD = 16, 8
HG = 4
GROUPS = HEADS // HG
REP = 4
EXPERTS, FF = 8, 512
CHUNKS = FF // P
TOPK = 2
SLOT_TILES = 40
RING = 4
AHEAD = 5
EPS = 1e-5
RSQRT_SEED = 0x5F3759DF
NEWTON = 3
C_W1, C_W2, C_B1, C_B2 = 0, FF, 2 * FF, 2 * FF + CHUNKS
RECORD = C_B2 + D


class Steps:

    def __init__(self, engine, semaphore):
        self.engine, self.semaphore, self.count, self.turn = engine, semaphore, 0, 0

    def mark(self, instruction):
        instruction.then_inc(self.semaphore, 1)
        self.count += 1

    def settle(self):
        self.engine.wait_ge(self.semaphore, self.turn + self.count)

    def done(self, instruction):
        self.mark(instruction)
        self.settle()

    def enter(self, i, per_turn):
        self.turn, self.start, self.per_turn = i * per_turn, self.count, per_turn

    def leave(self, turns):
        assert self.count - self.start == self.per_turn, (self.count - self.start, self.per_turn)
        self.count, self.turn = self.start + turns * self.per_turn, 0


def wait(engine, semaphore, value):
    if not isinstance(value, int) or value > 0:
        engine.wait_ge(semaphore, value)


def macaron(nc, x, W1, b1, W2, b2, gamma, beta, router_w, router_b, w1, fb1, w2, fb2, out):
    ctx = ExitStack()
    with ctx:
        def sb(name, shape, dt=F32):
            return ctx.enter_context(nc.sbuf_tensor(name, shape, dt))

        def sem(name):
            return ctx.enter_context(nc.semaphore(name))

        xn_rows = nc.dram_tensor("xn_rows", [TOKENS, D], F32).ap()
        y_rows = nc.dram_tensor("y_rows", [TOPK * TOKENS + SLOT_TILES * P, D], F32).ap()

        ident = sb("ident", [P, P])
        ones = sb("ones", [P, P])
        ones_h = sb("ones_h", [P, P], BF16)
        before = sb("before", [P, P], BF16)
        iota = sb("iota", [P, P])
        token_id = sb("token_id", [P, TILES])
        rank_of = sb("rank_of", [P, EXPERTS])
        spare_row = sb("spare_row", [P, SLOT_TILES])
        quarter = sb("quarter", [P, HG])
        ones8 = sb("ones8", [P, EXPERTS])
        records = sb("records", [P, EXPERTS, RECORD])
        row = sb("row", [1, EXPERTS * D + EXPERTS + 2 * D + D])
        rw = sb("rw", [P, EXPERTS])
        rb_all = sb("rb_all", [P, EXPERTS])
        uvb_all = sb("uvb_all", [P, 2 * D])
        w_in = sb("w_in", [P, 4 * D])
        w_in_hi = sb("w_in_hi", [P, 4 * D], F32R)
        w_in_lo = sb("w_in_lo", [P, 4 * D], F32R)
        w_out = sb("w_out", [P, D])
        w_out_g = sb("w_out_g", [P, D])
        cols = sb("cols", [P, 6])
        beta_all = sb("beta_all", [P, P])
        yb_all = sb("yb_all", [P, D])
        spread = sb("spread", [P, 4, GROUPS, P], F32R)

        X = sb("X", [P, TILES, D])
        stats = sb("stats", [P, TILES, 6])
        mean = sb("mean", [P, TILES])
        rstd = sb("rstd", [P, TILES])
        scr = [sb(f"scr{i}", [P, TILES]) for i in range(5)]

        LG = sb("LG", [P, TILES, EXPERTS])
        one_hot = sb("one_hot", [P, TOPK, TILES, EXPERTS])
        weighed = sb("weighed", [P, TILES, EXPERTS])
        chosen_place = sb("chosen_place", [P, TOPK, TILES, EXPERTS])
        top = sb("top", [P, TOPK, TILES])
        first = sb("first", [P, TILES])
        half_gate = sb("half_gate", [P, TOPK, TILES])
        chosen = sb("chosen", [P, TILES, EXPERTS], BF16)
        running = sb("running", [P, 1 + EXPERTS * TILES])
        place = sb("place", [P, EXPERTS, TILES])
        n_int = sb("n_int", [P, EXPERTS], I32)
        n_tiles = sb("n_tiles", [P, EXPERTS])
        n_upto = sb("n_upto", [P, EXPERTS])
        base = sb("base", [P, EXPERTS])
        te_cmp = sb("te_cmp", [1, SLOT_TILES, EXPERTS])
        te_sum = sb("te_sum", [1, SLOT_TILES])
        tile_expert = sb("tile_expert", [1, SLOT_TILES], I32)
        slot_i = sb("slot_i", [P, TOPK * TILES], I32)
        slot_f = sb("slot_f", [P, TOPK * TILES])
        slot_lo_i = sb("slot_lo_i", [P, TOPK * TILES], I32)
        slot_hi_i = sb("slot_hi_i", [P, TOPK * TILES], I32)
        region = sb("region", [P, TILES * TOPK * D])
        YL = region[:].rearrange("p (t j d) -> p t j d", j=TOPK, d=D)
        A = region[:].rearrange("p (n j q) -> p n j q", j=HG, q=SEQ)
        halves, N = region[:].bitcast(F16), TOPK * TILES
        in_tile = halves[:, 0:N * P].rearrange("p (n s) -> p n s", n=N)
        tile_hot = halves[:, N * P:N * (P + SLOT_TILES)].rearrange("p (n s) -> p n s", n=N)
        tile_load = halves[:, N * (P + SLOT_TILES):N * (P + 3 * SLOT_TILES)].rearrange(
            "p (n a s) -> p n a s", n=N, a=2)
        slot_map = sb("slot_map", [P, 2, SLOT_TILES])
        dst_f = sb("dst_f", [P, SLOT_TILES])
        src_row = sb("src_row", [P, SLOT_TILES], U32)
        dst_row = sb("dst_row", [P, SLOT_TILES], U32)

        src_s = [sb(f"src_s{k}", [P, 1], U32) for k in range(RING)]
        dst_s = [sb(f"dst_s{k}", [P, 1], U32) for k in range(RING)]
        XG = sb("XG", [P, RING, D])
        XT = sb("XT", [P, RING, P])
        WB = sb("WB", [P, RING, RECORD])
        HT = sb("HT", [P, 2, CHUNKS, P])
        YG = sb("YG", [P, RING, D])

        XTr = HT[:].rearrange("p a c q -> p a (c q)")

        XA = sb("XA", [P, TPB, D])
        xt_hi = sb("xt_hi", [P, SEQ], F32R)
        xt_lo = sb("xt_lo", [P, SEQ], F32R)
        QK = sb("QK", [P, 2, SEQ])
        qk_hi = sb("qk_hi", [P, 2, SEQ], F32R)
        qk_lo = sb("qk_lo", [P, 2, SEQ], F32R)
        uv_pre = sb("uv_pre", [P, TPB, 2 * D])
        U = sb("U", [P, TILES, D])
        XN = U
        VP = sb("VP", [P, 2, TPB, D + 32])
        KS = sb("KS", [P, 2, GROUPS, SEQ], F32R)
        QS = sb("QS", [P, GROUPS, SEQ])
        QM = sb("QM", [P, 2, GROUPS, HG, SEQ], F32R)
        AT = sb("AT", [P, GROUPS, SEQ])
        Z = sb("Z", [P, TPB, D])
        YT = sb("YT", [P, TPB, P])
        zst = sb("zst", [P, TPB, 6])
        z_sum = sb("z_sum", [P, TPB])
        z_diff = sb("z_diff", [P, TPB])
        z_var = sb("z_var", [P, TPB])
        z_half = sb("z_half", [P, TPB])
        z_step = sb("z_step", [P, TPB])
        z_rstd = sb("z_rstd", [P, TPB])
        Y = sb("Y", [P, TPB, D])
        PS = ctx.enter_context(nc.psum_tensor("PS", [P, 8, 512], F32))

        names = """made passed loaded router_in  bias_ps bias_out set_up spread_zero dve_own
            ln_x xn_ready xn_t_ps xn_t logits_ps tops_diff exp_top chosen_made counts_ps
            load_made map_ps src_staged xg_t_ps xt_ready w_staged up_ps gelu_out down_ps y_ready y_loaded
            dst_staged x_out xn_attn xa_ready x_biased xt_ps xt_split qk_ps qk_act uv_ps uv_biased uv_act qk_split rep_ps rep_out qm_ready
            s_ps s_act av_ps at_out z_ps z_gated z_centred yt_ps yt_out y_ps y_out stored stored_xn""".split()
        S = {n: sem(n) for n in names}
        gathered = [sem(f"gathered{k}") for k in range(RING)]
        scattered = [sem(f"scattered{k}") for k in range(RING)]
        y_back = [sem(f"y_back{k}") for k in range(4)]
        w_loads = [sem(f"w_loads{k}") for k in range(2)]
        x_in = [sem(f"x_in{k}") for k in range(4)]
        made, loaded, bias_ps, bias_out, set_up, spread_zero, router_in = (
            S[n] for n in ("made", "loaded", "bias_ps", "bias_out", "set_up", "spread_zero", "router_in"))

        LOADS = 9
        MADE = 16
        x_t = x.rearrange("(t p) d -> p t d", p=P)
        out_t = out.rearrange("(t p) d -> p t d", p=P)
        R_B2, R_RB, R_UV, R_YB = 0, EXPERTS * D, EXPERTS * D + EXPERTS, EXPERTS * D + EXPERTS + 2 * D
        OWN_PER_PAIR = 2 * 17
        QTR = TILES // 4

        block = ctx.enter_context(nc.Block())

        @block.sync
        def _(sp):
            sp.dma_start(X[:, 0:QTR, :], x_t[:, 0:QTR, :]).then_inc(x_in[0], 16)
            sp.dma_start(rw[:], router_w).then_inc(router_in, 16)
            sp.dma_start(row[:, R_RB:R_UV], router_b.rearrange("(a e) -> a e", a=1)).then_inc(router_in, 16)
            for k in range(1, 4):
                sp.dma_start(X[:, k * QTR:(k + 1) * QTR, :], x_t[:, k * QTR:(k + 1) * QTR, :]).then_inc(x_in[k], 16)
            sp.wait_ge(x_in[3], 16)
            sp.dma_start(records[:, :, C_B1:C_B2], fb1.rearrange("e (p c) -> p e c", p=P)).then_inc(w_loads[0], 16)
            sp.dma_start(records[:, :, C_W1:C_W2], w1.rearrange("e d f -> d e f")).then_inc(w_loads[0], 16)
            sp.dma_start(records[:, :, C_W2:C_B1], w2.rearrange("e (p c) d -> p e (c d)", p=P)).then_inc(w_loads[1], 16)

            def ffn(f):
                for c in range(4):
                    sp.wait_ge(S["xn_ready"], 4 * f + c + 1)
                    sp.dma_start(xn_rows[c * QTR * P:(c + 1) * QTR * P, :].rearrange("(t p) d -> p t d", p=P),
                                 XN[:, c * QTR:(c + 1) * QTR, :]).then_inc(S["stored_xn"], 16)
                for k in range(RING):
                    sp.wait_ge(scattered[k], 16 * (f + 1) * SLOT_TILES // RING)
                for c in range(4):
                    rows = y_rows[c * QTR * P * TOPK:(c + 1) * QTR * P * TOPK, :]
                    sp.dma_start(YL[:, c * QTR:(c + 1) * QTR, :, :],
                                 rows.rearrange("(t p j) d -> p t j d", p=P, j=TOPK)).then_inc(y_back[c], 16)

            ffn(0)
            ffn(1)
            for c in range(4):
                sp.wait_ge(S["x_out"], 4 + (c + 1))
                sp.dma_start(out_t[:, c * QTR:(c + 1) * QTR, :], X[:, c * QTR:(c + 1) * QTR, :]).then_inc(S["stored"], 16)
            sp.wait_ge(S["stored"], 64)

        @block.gpsimd
        def _(pool):
            def make(ins):
                ins.then_inc(made, 1)

            make(pool.memset(ident[:], 0.0))
            make(pool.memset(before[:], 1.0))
            make(pool.memset(ones[:], 1.0))
            make(pool.memset(ones_h[:], 1.0))
            make(pool.memset(quarter[:], 1.0))
            make(pool.memset(ones8[:], 1.0))
            make(pool.iota(iota[:], pattern=[[1, P]], base=0, channel_multiplier=0,
                           allow_small_or_imprecise_dtypes=True))
            make(pool.iota(token_id[:], pattern=[[P, TILES]], base=0, channel_multiplier=1,
                           allow_small_or_imprecise_dtypes=True))
            make(pool.iota(rank_of[:], pattern=[[-1, EXPERTS]], base=EXPERTS, channel_multiplier=0,
                           allow_small_or_imprecise_dtypes=True))
            make(pool.iota(spare_row[:], pattern=[[P, SLOT_TILES]], base=TOPK * TOKENS + 1, channel_multiplier=1,
                           allow_small_or_imprecise_dtypes=True))
            make(pool.memset(running[:, 0:1], 0.0))
            pool.wait_ge(made, 11)
            make(pool.affine_select(out=ident[:], in_=ident[:], compare_op=ALU.not_equal, fill=1.0, base=0,
                                    pattern=[[-1, P]], channel_multiplier=1))
            make(pool.affine_select(out=before[:], in_=before[:], compare_op=ALU.is_gt, fill=0.0, base=0,
                                    pattern=[[1, P]], channel_multiplier=-1))
            make(pool.memset(VP[:, :, :, D:D + 32], 0.0))
            make(pool.affine_select(out=quarter[:], in_=quarter[:], compare_op=ALU.is_ge, fill=0.0, base=0,
                                    pattern=[[-32, HG]], channel_multiplier=1))
            pool.wait_ge(made, MADE - 1)
            make(pool.affine_select(out=quarter[:], in_=quarter[:], compare_op=ALU.is_ge, fill=0.0, base=31,
                                    pattern=[[32, HG]], channel_multiplier=-1))
            pool.memset(spread[:].bitcast(F32), 0.0).then_inc(spread_zero, 1)
            pool.wait_ge(loaded, 16 * LOADS)
            pool.tensor_copy(beta_all[:], cols[:, 1:2].to_broadcast([P, P])).then_inc(set_up, 1)
            pool.tensor_scalar(w_out_g[:], w_out[:], cols[:, 0:1], 1.0, ALU.mult, ALU.mult).then_inc(set_up, 1)
            pool.tensor_copy(w_in_hi[:], w_in[:]).then_inc(set_up, 1)
            pool.wait_ge(set_up, 3)
            pool.tensor_tensor(w_in_lo[:], w_in[:], w_in_hi[:].bitcast(F32), ALU.subtract).then_inc(set_up, 1)
            pool.wait_ge(spread_zero, 1)
            pool.wait_ge(made, MADE)
            picks = ident[:].rearrange("p (h d) -> p h d", d=HD)
            for part, copies in enumerate(((0, 1), (2, 3), (0, 2), (1, 3))):
                to = spread[:, part, :, :].rearrange("p g (j r d) -> p (g j) r d", r=REP, d=HD)
                for r in copies:
                    last = pool.tensor_copy(to[:, :, r, :], picks)
            last.then_inc(set_up, 1)

            def ffn(f):
                n0, r0 = f * SLOT_TILES, f * (SLOT_TILES // RING)

                def gather(s, k):
                    pool.wait_ge(S["src_staged"], s + (n0 + 1))
                    pool.sem_inc(S["passed"], 1)
                    pool.indirect_dma_start(XG[:, k, :], None, xn_rows,
                                            bass.IndirectOffsetOnAxis(ap=src_s[k][:], axis=0)).then_inc(gathered[k], 16)

                def scatter(s, k):
                    pool.wait_ge(S["y_ready"], s + (n0 + 1))
                    pool.sem_inc(S["passed"], 1)
                    pool.indirect_dma_start(y_rows, bass.IndirectOffsetOnAxis(ap=dst_s[k][:], axis=0),
                                            YG[:, k, :], None).then_inc(scattered[k], 16)

                def group(g, is_last=False, before_last=False):
                    for k in range(RING):
                        if not is_last and not (before_last and k + AHEAD >= 2 * RING):
                            gather(g * RING + k + AHEAD, (k + AHEAD) % RING)
                        scatter(g * RING + k, k)

                pool.wait_ge(S["stored_xn"], 64 * (f + 1))
                for s in range(AHEAD):
                    gather(s, s % RING)
                group(0)
                with pool.Fori(1, SLOT_TILES // RING - 2) as g:
                    group(g)
                group(SLOT_TILES // RING - 2, before_last=True)
                group(SLOT_TILES // RING - 1, is_last=True)

            def masks(b, par):
                for r in range(2):
                    pool.wait_ge(S["rep_out"], b * 4 + (r + 1))
                    if r == 0:
                        wait(pool, S["s_ps"], (b - 1) * 8)
                    pool.sem_inc(S["passed"], 1)
                    for j in range(HG):
                        last = pool.tensor_scalar(QM[:, par, 2 * r:2 * r + 2, j, :], QS[:, 2 * r:2 * r + 2, :],
                                                  quarter[:, j:j + 1], 1.0, ALU.mult, ALU.mult)
                    last.then_inc(S["qm_ready"], 1)

            def prepare(b):
                wait(pool, S["xt_ps"], b)
                pool.sem_inc(S["passed"], 1)
                pool.tensor_copy(XA[:], XN[:, bass.ds(b * TPB, TPB), :]).then_inc(S["xa_ready"], 1)

            ffn(0)
            pool.wait_ge(S["xn_attn"], 1)
            prepare(0)
            pool.wait_ge(S["xn_attn"], 2)
            prepare(1)
            masks(0, 0)
            pool.tensor_tensor(X[:], X[:], yb_all[:].unsqueeze(1).to_broadcast([P, TILES, D]), ALU.add
                               ).then_inc(S["x_biased"], 1)
            prepare(2)
            masks(1, 1)
            with pool.Fori(1, BATCH // 2 - 1) as i:
                prepare(i * 2 + 1)
                masks(i * 2, 0)
                prepare(i * 2 + 2)
                masks(i * 2 + 1, 1)
            prepare(BATCH - 1)
            masks(BATCH - 2, 0)
            masks(BATCH - 1, 1)
            ffn(1)

        @block.tensor
        def _(pe):
            pe.wait_ge(made, MADE)
            pe.wait_ge(router_in, 32)
            pe.matmul(PS[:, 3, 0:EXPERTS], ones[0:1, :], row[:, R_RB:R_UV], start=True, stop=True).then_inc(bias_ps, 1)

            def biases():
                pe.wait_ge(loaded, 16 * LOADS)
                pe.wait_ge(S["xn_t"], 4)
                for h in range(2):
                    pe.matmul(PS[:, h, :], ones[0:1, :], row[:, 512 * h:512 * h + 512],
                              start=True, stop=True).then_inc(bias_ps, 1)
                pe.matmul(PS[:, 2, 0:2 * D], ones[0:1, :], row[:, R_UV:R_YB], start=True, stop=True)
                pe.wait_ge(set_up, 1)
                pe.matmul(PS[:, 2, 2 * D:3 * D], beta_all[:], w_out[:], start=True, stop=False)
                pe.matmul(PS[:, 2, 2 * D:3 * D], ones[0:1, :], row[:, R_YB:R_YB + D], start=False, stop=True
                          ).then_inc(bias_ps, 1)

            def ffn(f):
                n0 = f * SLOT_TILES

                def turn_rows(c):
                    pe.wait_ge(S["xn_ready"], 4 * f + c + 1)
                    wait(pe, S["xn_t"], 4 * f + c - 1)
                    for k in range(QTR):
                        mm = pe.transpose(PS[:, c % 2, k * P:(k + 1) * P], XN[:, c * QTR + k, :], ident[:])
                    mm.then_inc(S["xn_t_ps"], 1)

                turn_rows(0)
                for c in range(4):
                    if c < 3:
                        turn_rows(c + 1)
                    pe.wait_ge(S["xn_t"], 4 * f + c + 1)
                    for k in range(QTR):
                        t = c * QTR + k
                        mm = pe.matmul(PS[:, 4, t * EXPERTS:(t + 1) * EXPERTS], XTr[:, c % 2, k * P:(k + 1) * P], rw[:],
                                       start=True, stop=True)
                    mm.then_inc(S["logits_ps"], 1)
                if f == 0:
                    biases()
                pe.wait_ge(S["chosen_made"], f + 1)
                every = chosen[:].rearrange("p t e -> p e t")
                pe.matmul(PS[:, 6, 0:P], before[:], every, start=True, stop=True)
                pe.matmul(PS[:, 7, 0:P], ones_h[:], every, start=True, stop=True).then_inc(S["counts_ps"], 1)
                pe.wait_ge(S["load_made"], f + 1)
                for n in range(TOPK * TILES):
                    mm = pe.matmul(PS[:, 5, 0:2 * SLOT_TILES], in_tile[:, n, :],
                                   tile_load[:, n, :, :].rearrange("p a s -> p (a s)"),
                                   start=(n == 0), stop=(n == TOPK * TILES - 1))
                mm.then_inc(S["map_ps"], 1)

                if f == 0:
                    pe.wait_ge(bias_out, 5)

                def turn(s, k, g):
                    pe.wait_ge(gathered[k], (g + (f * SLOT_TILES // RING + 1)) * 16)
                    wait(pe, S["xt_ready"], s + (n0 - 1))
                    pe.transpose(PS[:, k % 2, 0:P], XG[:, k, :], ident[:]).then_inc(S["xg_t_ps"], 1)

                def up(s, k):
                    pe.wait_ge(S["xt_ready"], s + (n0 + 1))
                    pe.wait_ge(S["w_staged"], s + (n0 + 1))
                    wait(pe, S["gelu_out"], (s + (n0 - 1)) * CHUNKS)
                    for c in range(CHUNKS):
                        mm = pe.matmul(PS[:, 2 + k % 2, c * P:(c + 1) * P], WB[:, k, C_W1 + c:C_W1 + FF:CHUNKS],
                                       XT[:, k, :], start=True, stop=True)
                    mm.then_inc(S["up_ps"], 1)

                def down(s, k):
                    wait(pe, S["y_ready"], s + (n0 - 1))
                    for c in range(CHUNKS):
                        pe.wait_ge(S["gelu_out"], (s + n0) * CHUNKS + (c + 1))
                        mm = pe.matmul(PS[:, 4 + k % 2, 0:D], HT[:, k % 2, c, :],
                                       WB[:, k, C_W2 + c * D:C_W2 + (c + 1) * D],
                                       start=(c == 0), stop=(c == CHUNKS - 1))
                    mm.then_inc(S["down_ps"], 1)

                def group(g, is_last):
                    for k in range(RING):
                        if not (is_last and k + 2 >= RING):
                            turn(g * RING + k + 2, (k + 2) % RING, g + (k + 2) // RING)
                        if not (is_last and k + 1 >= RING):
                            up(g * RING + k + 1, (k + 1) % RING)
                        down(g * RING + k, k)

                turn(0, 0, 0)
                turn(1, 1, 0)
                up(0, 0)
                group(0, False)
                with pe.Fori(1, SLOT_TILES // RING - 1) as g:
                    group(g, False)
                group(SLOT_TILES // RING - 1, True)

            def project(b, part):
                if part == "turn":
                    pe.wait_ge(S["xa_ready"], b + 1)
                    if isinstance(b, int) and b < 3:
                        wait(pe, S["rep_out"], 4 * (b - 1) + 3)
                    else:
                        pe.wait_ge(S["yt_out"], b - 2)
                    for t in range(TPB):
                        mm = pe.transpose(PS[:, 5, t * P:(t + 1) * P], XA[:, t, :], ident[:])
                    mm.then_inc(S["xt_ps"], 1)
                elif part == "qk":
                    pe.wait_ge(S["xt_split"], b + 1)
                    if isinstance(b, int) and b < 3:
                        wait(pe, S["rep_out"], 4 * b)
                    else:
                        pe.wait_ge(S["y_out"], b - 2)
                    for c in range(2):
                        q = slice((2 + c) * D, (3 + c) * D)
                        for n, (w, m) in enumerate(((w_in_hi, xt_hi), (w_in_hi, xt_lo), (w_in_lo, xt_hi))):
                            mm = pe.matmul(PS[:, 4, c * SEQ:(c + 1) * SEQ], w[:, q], m[:], start=(n == 0), stop=(n == 2))
                    mm.then_inc(S["qk_ps"], 1)
                else:
                    pe.wait_ge(S["rep_out"], b * 4 + 1)
                    wait(pe, S["z_gated"], b * 2 - 2)
                    for t in range(TPB):
                        q = slice(t * P, (t + 1) * P)
                        for n, (m, w) in enumerate(((xt_hi, w_in_hi), (xt_lo, w_in_hi), (xt_hi, w_in_lo))):
                            mm = pe.matmul(PS[:, 4, t * 2 * D:(t + 1) * 2 * D], m[:, q], w[:, 0:2 * D],
                                           start=(n == 0), stop=(n == 2))
                    mm.then_inc(S["uv_ps"], 1)

            def replicate(b, r):
                c, bank = r // 2, (4, 5, 5, 4)[r]
                if r == 0:
                    pe.wait_ge(S["qk_split"], b + 1)
                elif r == 1:
                    wait(pe, S["z_gated"], b * 2 - 3)
                elif r == 2:
                    pe.wait_ge(S["rep_out"], b * 4 + 2)
                else:
                    pe.wait_ge(S["uv_biased"], b + 1)
                for h in range(2):
                    g = 2 * (r % 2) + h
                    pe.matmul(PS[:, bank, h * SEQ:(h + 1) * SEQ], spread[:, 2 * c, g, :], qk_hi[:, c, :],
                              start=True, stop=False)
                    mm = pe.matmul(PS[:, bank, h * SEQ:(h + 1) * SEQ], spread[:, 2 * c + 1, g, :], qk_lo[:, c, :],
                                   start=False, stop=True)
                mm.then_inc(S["rep_ps"], 1)

            def scores(b, par, n):
                g, kt = n // 2, n % 2
                if n % 4 == 0:
                    pe.wait_ge(S["qm_ready"], b * 2 + (n // 4 + 1))
                    pe.wait_ge(S["rep_out"], b * 4 + (n // 4 + 3))
                wait(pe, S["s_act"], b * 8 + (n - 1))
                for h in range(2):
                    mm = pe.matmul(PS[:, 2 * (n % 2) + h, :], KS[:, par, g, kt * P:(kt + 1) * P],
                                   QM[:, par, g, 2 * h:2 * h + 2, :].rearrange("p j q -> p (j q)"),
                                   start=True, stop=True)
                mm.then_inc(S["s_ps"], 1)

            def attend(b, par, g):
                pe.wait_ge(S["uv_act"], b + 1)
                if g % 2 == 0:
                    wait(pe, S["at_out"], b * 2 + (g // 2 - 1))
                pe.wait_ge(S["s_act"], b * 8 + (2 * g + 2))
                for kt in range(TPB):
                    for j in range(HG):
                        h = (HG * g + j) * HD
                        mm = pe.matmul(PS[32 * j:32 * j + 32, 6 + g // 2, (g % 2) * SEQ:(g % 2 + 1) * SEQ],
                                       VP[:, par, kt, h:h + 32], A[:, (2 * g + kt) % 4, j, :],
                                       start=(kt == 0), stop=(kt == TPB - 1), tile_position=(0, 32 * j))
                mm.then_inc(S["av_ps"], 1)

            def back(b, t):
                if t == 0:
                    pe.wait_ge(S["at_out"], b * 2 + 2)
                if isinstance(b, int) and b >= BATCH - 2:
                    pe.wait_ge(S["y_out" if t else "yt_out"], b)
                elif t == 0:
                    pe.wait_ge(S["xt_split"], b + 3)
                else:
                    pe.wait_ge(S["rep_out"], b * 4 + 9)
                for g in range(GROUPS):
                    mm = pe.transpose(PS[:, 5 - t, g * P:(g + 1) * P], AT[:, g, t * P:(t + 1) * P], ident[:])
                mm.then_inc(S["z_ps"], 1)

            def output(b, part):
                if part == "turn":
                    pe.wait_ge(S["z_centred"], b + 1)
                    if not isinstance(b, int) or b < BATCH - 2:
                        pe.wait_ge(S["rep_out"], b * 4 + 11)
                    for t in range(TPB):
                        mm = pe.transpose(PS[:, 5, t * P:(t + 1) * P], Z[:, t, :], ident[:])
                    mm.then_inc(S["yt_ps"], 1)
                else:
                    pe.wait_ge(S["yt_out"], b + 1)
                    if not isinstance(b, int) or b < BATCH - 2:
                        pe.wait_ge(S["rep_out"], b * 4 + 12)
                    for t in range(TPB):
                        mm = pe.matmul(PS[:, 4, t * D:(t + 1) * D], YT[:, t, :], w_out_g[:], start=True, stop=True)
                    mm.then_inc(S["y_ps"], 1)

            def step(b, par, older=True, newer=2):
                scores(b, par, 0)
                scores(b, par, 1)
                if older:
                    attend(b - 1, 1 - par, 3)
                scores(b, par, 2)
                if newer:
                    replicate(b + 1, 0)
                attend(b, par, 0)
                if older:
                    back(b - 1, 0)
                scores(b, par, 3)
                if older:
                    back(b - 1, 1)
                if newer:
                    replicate(b + 1, 1)
                scores(b, par, 4)
                if newer:
                    project(b + 1, "uv")
                attend(b, par, 1)
                if newer:
                    replicate(b + 1, 2)
                scores(b, par, 5)
                if newer:
                    replicate(b + 1, 3)
                if older:
                    output(b - 1, "turn")
                scores(b, par, 6)
                if newer > 1:
                    project(b + 2, "turn")
                attend(b, par, 2)
                if older:
                    output(b - 1, "out")
                scores(b, par, 7)
                if newer > 1:
                    project(b + 2, "qk")

            def attention():
                pe.wait_ge(S["y_ready"], SLOT_TILES)
                pe.wait_ge(S["gelu_out"], SLOT_TILES * CHUNKS)
                pe.wait_ge(set_up, 5)
                project(0, "turn")
                project(0, "qk")
                replicate(0, 0)
                replicate(0, 1)
                project(0, "uv")
                replicate(0, 2)
                replicate(0, 3)
                project(1, "turn")
                project(1, "qk")
                step(0, 0, older=False)
                step(1, 1)
                with pe.Fori(1, BATCH // 2 - 1) as i:
                    step(i * 2, 0)
                    step(i * 2 + 1, 1)
                step(BATCH - 2, 0, newer=1)
                step(BATCH - 1, 1, newer=0)
                b = BATCH - 1
                attend(b, 1, 3)
                back(b, 0)
                back(b, 1)
                output(b, "turn")
                output(b, "out")

            ffn(0)
            attention()
            ffn(1)

        @block.scalar
        def _(act):
            act.dma_start(row[:, R_B2:R_RB], fb2.rearrange("(a e) d -> a (e d)", a=1)).then_inc(loaded, 16)
            act.dma_start(row[:, R_UV:R_YB], b1[0:2 * D].rearrange("(a e) -> a e", a=1)).then_inc(loaded, 16)
            act.dma_start(row[:, R_YB:R_YB + D], b2.rearrange("(a e) -> a e", a=1)).then_inc(loaded, 16)
            act.dma_start(cols[:, 0:1], gamma.rearrange("(p a) -> p a", a=1)).then_inc(loaded, 16)
            act.dma_start(cols[:, 1:2], beta.rearrange("(p a) -> p a", a=1)).then_inc(loaded, 16)
            for c in (2, 3):
                act.dma_start(cols[:, 2 + c:3 + c],
                              b1[c * D:(c + 1) * D].rearrange("(p a) -> p a", a=1)).then_inc(loaded, 16)
            act.dma_start(w_in[:], W1).then_inc(loaded, 16)
            act.dma_start(w_out[:], W2).then_inc(loaded, 16)
            act.wait_ge(bias_ps, 1)
            act.copy(rb_all[:], PS[:, 3, 0:EXPERTS]).then_inc(bias_out, 1)

            def ffn(f):
                n0 = f * SLOT_TILES
                for c in range(4):
                    act.wait_ge(S["xn_t_ps"], 4 * f + c + 1)
                    wait(act, S["logits_ps"], 4 * f + c - 1)
                    act.copy(XTr[:, c % 2, :], PS[:, c % 2, :]).then_inc(S["xn_t"], 1)
                if f == 0:
                    for h in range(2):
                        act.wait_ge(bias_ps, h + 2)
                        act.copy(records[:, 4 * h:4 * h + 4, C_B2:RECORD],
                                 PS[:, h, :].rearrange("p (e d) -> p e d", d=D)).then_inc(bias_out, 1)
                    act.wait_ge(bias_ps, 4)
                    act.copy(uvb_all[:], PS[:, 2, 0:2 * D]).then_inc(bias_out, 1)
                    act.copy(yb_all[:], PS[:, 2, 2 * D:3 * D]).then_inc(bias_out, 1)
                act.wait_ge(S["tops_diff"], f + 1)
                act.activation(scr[1][:], scr[0][:], ACT.Exp).then_inc(S["exp_top"], 1)

                def gelu(s, k):
                    wait(act, S["down_ps"], s + (n0 - 1))
                    act.wait_ge(S["up_ps"], s + (n0 + 1))
                    for c in range(CHUNKS):
                        act.activation(HT[:, k % 2, c, :], PS[:, 2 + k % 2, c * P:(c + 1) * P], ACT.Gelu,
                                       bias=WB[:, k, C_B1 + c:C_B1 + c + 1]).then_inc(S["gelu_out"], 1)

                for k in range(RING):
                    gelu(k, k)
                with act.Fori(1, SLOT_TILES // RING) as g:
                    for k in range(RING):
                        gelu(g * RING + k, k)

            def silu_scores(b, n):
                act.wait_ge(S["s_ps"], b * 8 + (n + 1))
                if n % 2 == 0:
                    wait(act, S["av_ps"], b * 4 + (n // 2 - 1))
                act.activation(A[:, n % 4, :, :].rearrange("p j q -> p (j q)"),
                               PS[:, 2 * (n % 2):2 * (n % 2) + 2, :].rearrange("p a q -> p (a q)"),
                               ACT.Silu).then_inc(S["s_act"], 1)

            def silu_qk(b):
                act.wait_ge(S["qk_ps"], b + 1)
                wait(act, S["qk_split"], b)
                for c in range(2):
                    a = act.activation(QK[:, c, :], PS[:, 4, c * SEQ:(c + 1) * SEQ], ACT.Silu, bias=cols[:, 4 + c:5 + c])
                a.then_inc(S["qk_act"], 1)

            def silu_uv(b, par):
                act.wait_ge(S["uv_biased"], b + 1)
                wait(act, S["av_ps"], (b - 1) * 4)
                act.activation(U[:, bass.ds(b * TPB, TPB), :], uv_pre[:, :, 0:D], ACT.Silu)
                act.activation(VP[:, par, :, 0:D], uv_pre[:, :, D:2 * D], ACT.Silu).then_inc(S["uv_act"], 1)

            def copy_keys(b, par, r):
                act.wait_ge(S["rep_ps"], b * 4 + (r + 1))
                wait(act, S["s_ps"], (b - 1) * 8)
                act.copy(KS[:, par, 2 * (r - 2):2 * (r - 1), :],
                         PS[:, 7 - r, :].rearrange("p (g q) -> p g q", g=2)).then_inc(S["rep_out"], 1)

            def step(b, par, newer=2):
                for n in range(5):
                    silu_scores(b, n)
                if newer:
                    copy_keys(b + 1, 1 - par, 2)
                silu_scores(b, 5)
                if newer:
                    copy_keys(b + 1, 1 - par, 3)
                silu_scores(b, 6)
                if newer:
                    silu_uv(b + 1, 1 - par)
                silu_scores(b, 7)
                if newer > 1:
                    silu_qk(b + 2)

            ffn(0)
            silu_qk(0)
            copy_keys(0, 0, 2)
            copy_keys(0, 0, 3)
            silu_uv(0, 0)
            silu_qk(1)
            step(0, 0)
            step(1, 1)
            with act.Fori(1, BATCH // 2 - 1) as i:
                step(i * 2, 0)
                step(i * 2 + 1, 1)
            step(BATCH - 2, 0, newer=1)
            step(BATCH - 1, 1, newer=0)
            ffn(1)

        @block.vector
        def _(dve):
            own = Steps(dve, S["dve_own"])
            link = own.done

            def ln_coefficients(st, mu, rs, w):
                dve.tensor_tensor(w[1], st[:, :, 2], st[:, :, 5], ALU.add)
                dve.tensor_tensor(mu, st[:, :, 1], st[:, :, 4], ALU.add)
                link(dve.tensor_tensor(w[0], st[:, :, 1], st[:, :, 4], ALU.subtract))
                dve.tensor_scalar(w[1], w[1], 1.0 / D, EPS, ALU.mult, ALU.add)
                dve.tensor_scalar(mu, mu, 0.5, None, ALU.mult)
                link(dve.scalar_tensor_tensor(out=w[0], in0=w[0], scalar=0.25, in1=w[0], op0=ALU.mult, op1=ALU.mult))
                link(dve.tensor_tensor(w[1], w[1], w[0], ALU.add))
                dve.tensor_scalar(w[3], w[1], -0.5, None, ALU.mult)
                link(dve.tensor_scalar(rs.bitcast(I32), w[1].bitcast(I32), -0.5, float(RSQRT_SEED), ALU.mult, ALU.add))
                for _ in range(NEWTON):
                    link(dve.tensor_tensor(w[2], rs, rs, ALU.mult))
                    link(dve.tensor_tensor(w[2], w[2], w[3], ALU.mult))
                    link(dve.scalar_tensor_tensor(out=rs, in0=w[2], scalar=1.5, in1=rs, op0=ALU.add, op1=ALU.mult))

            def tile_stats(t):
                return dve.bn_stats(stats[:, t, :], X[:, t, :])

            def coefficients():
                ln_coefficients(stats[:], mean[:], rstd[:], [w[:] for w in scr])

            def normalize_rows(first_t, end_t):
                for t in range(first_t, end_t):
                    n = dve.tensor_scalar(XN[:, t, :], X[:, t, :], mean[:, t:t + 1], rstd[:, t:t + 1],
                                          ALU.subtract, ALU.mult)
                n.then_inc(S["xn_attn"], 1)

            def ffn(f):
                n0 = f * SLOT_TILES
                for t in range(TILES):
                    if f == 0 and t % QTR == 0:
                        dve.wait_ge(x_in[t // QTR], 16)
                    n = tile_stats(t)
                link(n)
                coefficients()
                for c in range(4):
                    for t in range(c * QTR, (c + 1) * QTR):
                        n = dve.tensor_scalar(XN[:, t, :], X[:, t, :], mean[:, t:t + 1], rstd[:, t:t + 1],
                                              ALU.subtract, ALU.mult)
                    n.then_inc(S["xn_ready"], 1)
                dve.wait_ge(S["logits_ps"], 4 * (f + 1))
                if f == 0:
                    dve.wait_ge(bias_out, 1)
                link(dve.tensor_tensor(LG[:], PS[:, 4, 0:TILES * EXPERTS].rearrange("p (t e) -> p t e", e=EXPERTS),
                                       rb_all[:].unsqueeze(1).to_broadcast([P, TILES, EXPERTS]), ALU.add))
                ranks = rank_of[:].unsqueeze(1).to_broadcast([P, TILES, EXPERTS])
                for j in range(TOPK):
                    link(dve.tensor_reduce(top[:, j, :], LG[:], AX.X, ALU.max))
                    link(dve.tensor_tensor(weighed[:], LG[:],
                                           top[:, j, :].unsqueeze(2).to_broadcast([P, TILES, EXPERTS]), ALU.is_equal))
                    link(dve.tensor_tensor(weighed[:], weighed[:], ranks, ALU.mult))
                    link(dve.tensor_reduce(first[:], weighed[:], AX.X, ALU.max))
                    link(dve.tensor_tensor(one_hot[:, j, :, :], ranks,
                                           first[:].unsqueeze(2).to_broadcast([P, TILES, EXPERTS]), ALU.is_equal))
                    if j == 0:
                        link(dve.scalar_tensor_tensor(out=LG[:], in0=one_hot[:, 0, :, :], scalar=-3.0e38, in1=LG[:],
                                                      op0=ALU.mult, op1=ALU.add))
                dve.tensor_tensor(scr[0][:], top[:, 1, :], top[:, 0, :], ALU.subtract).then_inc(S["tops_diff"], 1)
                dve.tensor_tensor(chosen[:], one_hot[:, 0, :, :], one_hot[:, 1, :, :], ALU.add).then_inc(S["chosen_made"], 1)
                dve.wait_ge(S["counts_ps"], f + 1)
                link(dve.tensor_tensor_scan(running[:, 1:], ones[:], PS[:, 7, 0:P], 0.0, ALU.mult, ALU.add))
                upto = running[:, 1:].rearrange("p (e t) -> p e t", t=TILES)
                earlier = running[:, 0:EXPERTS * TILES].rearrange("p (e t) -> p e t", t=TILES)
                ahead = PS[:, 6, 0:P].rearrange("p (e t) -> p e t", t=TILES)
                dve.tensor_tensor(place[:], earlier, ahead, ALU.add)
                link(dve.scalar_tensor_tensor(out=n_int[:], in0=upto[:, :, TILES - 1], scalar=float(P - 1),
                                              in1=earlier[:, :, 0], op0=ALU.add, op1=ALU.subtract))
                link(dve.tensor_scalar(n_int[:], n_int[:], 7, None, ALU.logical_shift_right))
                link(dve.tensor_copy(n_tiles[:], n_int[:]))
                link(dve.tensor_tensor_scan(n_upto[:], ones8[:], n_tiles[:], 0.0, ALU.mult, ALU.add))
                link(dve.tensor_tensor(base[:], n_upto[:], n_tiles[:], ALU.subtract))
                link(dve.scalar_tensor_tensor(out=base[:], in0=base[:], scalar=float(P), in1=earlier[:, :, 0],
                                              op0=ALU.mult, op1=ALU.subtract))
                link(dve.tensor_tensor(place[:], place[:], base[:].unsqueeze(2).to_broadcast([P, EXPERTS, TILES]), ALU.add))
                link(dve.tensor_tensor(chosen_place[:], one_hot[:], place[:].rearrange("p e t -> p t e").unsqueeze(1)
                                       .to_broadcast([P, TOPK, TILES, EXPERTS]), ALU.mult))
                link(dve.tensor_reduce(slot_f[:], chosen_place[:].rearrange("p j t e -> p (j t) e"), AX.X, ALU.add))
                link(dve.tensor_copy(slot_i[:], slot_f[:]))
                dve.tensor_scalar(slot_lo_i[:], slot_i[:], P - 1, None, ALU.bitwise_and)
                link(dve.tensor_scalar(slot_hi_i[:], slot_i[:], 7, None, ALU.logical_shift_right))
                N = TOPK * TILES
                link(dve.tensor_tensor(tile_hot, iota[:, 0:SLOT_TILES].unsqueeze(1).to_broadcast([P, N, SLOT_TILES]),
                                       slot_hi_i[:].unsqueeze(2).to_broadcast([P, N, SLOT_TILES]), ALU.is_equal))
                for j in range(TOPK):
                    q = slice(j * TILES, (j + 1) * TILES)
                    link(dve.tensor_tensor(tile_load[:, q, 0, :], tile_hot[:, q, :],
                                           token_id[:].unsqueeze(2).to_broadcast([P, TILES, SLOT_TILES]), ALU.mult))
                    link(dve.tensor_scalar(tile_load[:, q, 1, :], tile_hot[:, q, :], float(j + 1), None, ALU.mult))
                dve.tensor_tensor(in_tile, iota[:].unsqueeze(1).to_broadcast([P, N, P]),
                                  slot_lo_i[:].unsqueeze(2).to_broadcast([P, N, P]), ALU.is_equal).then_inc(S["load_made"], 1)
                dve.wait_ge(S["exp_top"], f + 1)
                link(dve.tensor_scalar(scr[2][:], scr[1][:], 1.0, None, ALU.add))
                link(dve.reciprocal(scr[3][:], scr[2][:]))
                link(dve.tensor_scalar(half_gate[:, 0, :], scr[3][:], 0.5, None, ALU.mult))
                link(dve.tensor_tensor(half_gate[:, 1, :], half_gate[:, 0, :], scr[1][:], ALU.mult))
                link(dve.tensor_tensor(te_cmp[:], iota[0:1, 0:SLOT_TILES].unsqueeze(2).to_broadcast([1, SLOT_TILES, EXPERTS]),
                                       n_upto[0:1, :].unsqueeze(1).to_broadcast([1, SLOT_TILES, EXPERTS]), ALU.is_ge))
                link(dve.tensor_reduce(te_sum[:], te_cmp[:], AX.X, ALU.add))
                link(dve.tensor_scalar(tile_expert[:], te_sum[:], float(EXPERTS - 1), None, ALU.min))
                dve.wait_ge(S["map_ps"], f + 1)
                link(dve.tensor_copy(slot_map[:], PS[:, 5, 0:2 * SLOT_TILES].rearrange("p (a s) -> p a s", a=2)))
                link(dve.tensor_copy(src_row[:], slot_map[:, 0, :]))
                link(dve.tensor_scalar(dst_f[:], slot_map[:, 1, :], 0.0, None, ALU.is_equal))
                link(dve.tensor_tensor(dst_f[:], dst_f[:], spare_row[:], ALU.mult))
                link(dve.scalar_tensor_tensor(out=dst_f[:], in0=dst_f[:], scalar=-1.0, in1=slot_map[:, 1, :],
                                              op0=ALU.add, op1=ALU.add))
                link(dve.scalar_tensor_tensor(out=dst_row[:], in0=slot_map[:, 0, :], scalar=float(TOPK), in1=dst_f[:],
                                              op0=ALU.mult, op1=ALU.add))

                def stage_src(s, k):
                    wait(dve, S["xg_t_ps"], s + (n0 - 3))
                    dve.tensor_copy(src_s[k][:], src_row[:, bass.ds(s, 1)]).then_inc(S["src_staged"], 1)

                def stage_weights(s, k):
                    wait(dve, S["y_ready"], s + (n0 - 3))
                    e = dve.value_load(tile_expert[0:1, bass.ds(s, 1)], min_val=0, max_val=EXPERTS - 1)
                    dve.tensor_copy(WB[:, k, :], records[:, bass.ds(e, 1), :].rearrange("p a r -> p (a r)")
                                    ).then_inc(S["w_staged"], 1)

                def evacuate_x(s, k):
                    dve.wait_ge(S["xg_t_ps"], s + (n0 + 1))
                    wait(dve, S["up_ps"], s + (n0 - 3))
                    dve.tensor_copy(XT[:, k, :], PS[:, k % 2, 0:P]).then_inc(S["xt_ready"], 1)

                def evacuate_y(s, k, g):
                    wait(dve, scattered[k], (g + f * (SLOT_TILES // RING)) * 16)
                    dve.tensor_copy(dst_s[k][:], dst_row[:, bass.ds(s, 1)]).then_inc(S["dst_staged"], 1)
                    dve.wait_ge(S["down_ps"], s + (n0 + 1))
                    dve.wait_ge(S["w_staged"], s + (n0 + 1))
                    dve.tensor_tensor(YG[:, k, :], PS[:, 4 + k % 2, 0:D], WB[:, k, C_B2:RECORD], ALU.add
                                      ).then_inc(S["y_ready"], 1)

                def group(g, is_last=False, before_last=False):
                    for k in range(RING):
                        if not is_last and not (before_last and k + AHEAD >= 2 * RING):
                            stage_src(g * RING + k + AHEAD, (k + AHEAD) % RING)
                        if not (is_last and k + 2 >= RING):
                            evacuate_x(g * RING + k + 2, (k + 2) % RING)
                        evacuate_y(g * RING + k, k, g)
                        if not (is_last and k + 3 >= RING):
                            stage_weights(g * RING + k + 3, (k + 3) % RING)

                for s in range(RING):
                    stage_src(s, s)
                if f == 0:
                    for k in range(2):
                        dve.wait_ge(w_loads[k], 32 - 16 * k)
                for s in range(3):
                    stage_weights(s, s)
                for s in range(2):
                    evacuate_x(s, s)
                    if s + RING < AHEAD:
                        stage_src(s + RING, s)
                group(0)
                with dve.Fori(1, SLOT_TILES // RING - 2) as g:
                    group(g)
                group(SLOT_TILES // RING - 2, before_last=True)
                group(SLOT_TILES // RING - 1, is_last=True)
                if f == 0:
                    dve.wait_ge(loaded, 16 * LOADS)
                for c in range(4):
                    dve.wait_ge(y_back[c], (f + 1) * 16)
                    for j in range(TOPK):
                        for t in range(c * QTR, (c + 1) * QTR):
                            n = dve.scalar_tensor_tensor(out=X[:, t, :], in0=YL[:, t, j, :], scalar=half_gate[:, j, t:t + 1],
                                                         in1=X[:, t, :], op0=ALU.mult, op1=ALU.add)
                        if j == 0:
                            link(n)
                    n.then_inc(S["x_out"], 1)
                    if f == 0:
                        dve.wait_ge(S["x_out"], c + 1)
                        for t in range(c * QTR, (c + 1) * QTR):
                            n = tile_stats(t)
                        if c == 3:
                            link(n)
                if f == 0:
                    coefficients()
                    normalize_rows(0, TPB)

            def split_x(b):
                dve.wait_ge(S["xt_ps"], b + 1)
                wait(dve, S["uv_ps"], b)
                link(dve.tensor_copy(xt_hi[:], PS[:, 5, 0:SEQ]))
                dve.tensor_tensor(xt_lo[:], PS[:, 5, 0:SEQ], xt_hi[:].bitcast(F32), ALU.subtract).then_inc(S["xt_split"], 1)

            def split_qk_high(b):
                dve.wait_ge(S["qk_act"], b + 1)
                wait(dve, S["rep_ps"], b * 4)
                own.mark(dve.tensor_copy(qk_hi[:], QK[:]))

            def split_qk_low(b):
                own.settle()
                dve.tensor_tensor(qk_lo[:], QK[:], qk_hi[:].bitcast(F32), ALU.subtract).then_inc(S["qk_split"], 1)

            def bias_uv(b):
                dve.wait_ge(S["uv_ps"], b + 1)
                wait(dve, S["uv_act"], b)
                dve.tensor_tensor(uv_pre[:], PS[:, 4, :].rearrange("p (t d) -> p t d", t=TPB),
                                  uvb_all[:].unsqueeze(1).to_broadcast([P, TPB, 2 * D]), ALU.add).then_inc(S["uv_biased"], 1)

            def copy_queries(b, r):
                dve.wait_ge(S["rep_ps"], b * 4 + (r + 1))
                wait(dve, S["qm_ready"], b * 2 + (r - 1))
                dve.tensor_copy(QS[:, 2 * r:2 * r + 2, :], PS[:, 4 + r, :].rearrange("p (g q) -> p g q", g=2)
                                ).then_inc(S["rep_out"], 1)

            def copy_heads(b, h):
                dve.wait_ge(S["av_ps"], b * 4 + (2 * h + 2))
                wait(dve, S["z_ps"], b * 2)
                dve.tensor_copy(AT[:, 2 * h:2 * h + 2, :], PS[:, 6 + h, :].rearrange("p (g q) -> p g q", g=2)
                                ).then_inc(S["at_out"], 1)

            def gate(b, t):
                dve.wait_ge(S["z_ps"], b * 2 + (t + 1))
                if t == 0:
                    wait(dve, S["yt_ps"], b)
                heads = PS[:, 5 - t, :].rearrange("p (h r) -> p h r", r=32)[:, :, 0:HD]
                u = U[:, bass.ds(b * TPB + t, 1), :].rearrange("p a (h r) -> p (a h) r", r=HD)
                dve.scalar_tensor_tensor(out=Z[:, t, :].rearrange("p (h r) -> p h r", r=HD), in0=heads,
                                         scalar=0.5 / SEQ, in1=u, op0=ALU.mult, op1=ALU.mult).then_inc(S["z_gated"], 1)

            def z_stats(b):
                dve.wait_ge(S["z_gated"], b * 2 + 2)
                for t in range(TPB):
                    n = dve.bn_stats(zst[:, t, :], Z[:, t, :])
                own.mark(n)

            def z_sums():
                own.settle()
                dve.tensor_tensor(z_diff[:], zst[:, :, 1], zst[:, :, 4], ALU.subtract)
                dve.tensor_tensor(z_var[:], zst[:, :, 2], zst[:, :, 5], ALU.add)
                own.mark(dve.tensor_tensor(z_sum[:], zst[:, :, 1], zst[:, :, 4], ALU.add))

            def z_centre():
                own.settle()
                for t in range(TPB):
                    n = dve.tensor_scalar(Z[:, t, :], Z[:, t, :], 2.0, z_sum[:, t:t + 1], ALU.mult, ALU.subtract)
                n.then_inc(S["z_centred"], 1)
                dve.tensor_scalar(z_var[:], z_var[:], 4.0 / D, EPS, ALU.mult, ALU.add)
                own.mark(dve.tensor_tensor(z_diff[:], z_diff[:], z_diff[:], ALU.mult))

            def z_variance():
                own.settle()
                own.mark(dve.tensor_tensor(z_var[:], z_var[:], z_diff[:], ALU.add))

            def root_seed():
                own.settle()
                dve.tensor_scalar(z_half[:], z_var[:], -0.5, None, ALU.mult)
                own.mark(dve.tensor_scalar(z_rstd[:].bitcast(I32), z_var[:].bitcast(I32), -0.5, float(RSQRT_SEED),
                                           ALU.mult, ALU.add))

            def root_square():
                own.settle()
                own.mark(dve.tensor_tensor(z_step[:], z_rstd[:], z_rstd[:], ALU.mult))

            def root_scale():
                own.settle()
                own.mark(dve.tensor_tensor(z_step[:], z_step[:], z_half[:], ALU.mult))

            def root_refine():
                own.settle()
                own.mark(dve.scalar_tensor_tensor(out=z_rstd[:], in0=z_step[:], scalar=1.5, in1=z_rstd[:],
                                                  op0=ALU.add, op1=ALU.mult))

            def copy_yt(b):
                dve.wait_ge(S["yt_ps"], b + 1)
                wait(dve, S["y_ps"], b)
                dve.tensor_copy(YT[:], PS[:, 5, 0:SEQ].rearrange("p (t d) -> p t d", t=TPB)).then_inc(S["yt_out"], 1)

            def copy_y(b):
                dve.wait_ge(S["y_ps"], b + 1)
                dve.tensor_copy(Y[:], PS[:, 4, 0:TPB * D].rearrange("p (t d) -> p t d", t=TPB)).then_inc(S["y_out"], 1)

            def add_y(b):
                own.settle()
                dve.wait_ge(S["y_out"], b + 1)
                dve.wait_ge(S["x_biased"], 1)
                for t in range(TPB):
                    xt = X[:, bass.ds(b * TPB + t, 1), :].rearrange("p a d -> p (a d)")
                    n = dve.scalar_tensor_tensor(out=xt, in0=Y[:, t, :], scalar=z_rstd[:, t:t + 1], in1=xt,
                                                 op0=ALU.mult, op1=ALU.add)
                own.mark(n)

            def step(b, older=True, newer=2, root=True):
                if older:
                    copy_heads(b - 1, 1)
                if root:
                    root_square()
                if newer:
                    copy_queries(b + 1, 0)
                if root:
                    root_scale()
                if older:
                    gate(b - 1, 0)
                if root:
                    root_refine()
                if older:
                    gate(b - 1, 1)
                if root:
                    root_square()
                if older:
                    z_stats(b - 1)
                if newer:
                    copy_queries(b + 1, 1)
                if root:
                    root_scale()
                if older:
                    z_sums()
                if root:
                    root_refine()
                if root:
                    root_square()
                if newer:
                    bias_uv(b + 1)
                if older:
                    z_centre()
                if root:
                    root_scale()
                copy_heads(b, 0)
                if older:
                    z_variance()
                if root:
                    root_refine()
                if older:
                    copy_yt(b - 1)
                if newer > 1:
                    split_x(b + 2)
                if root:
                    add_y(b - 2)
                if older:
                    root_seed()
                    copy_y(b - 1)
                if newer > 1:
                    split_qk_high(b + 2)
                    split_qk_low(b + 2)

            def root():
                for _ in range(NEWTON):
                    root_square()
                    root_scale()
                    root_refine()

            def attention():
                split_x(0)
                normalize_rows(TPB, TILES)
                split_qk_high(0)
                split_qk_low(0)
                copy_queries(0, 0)
                copy_queries(0, 1)
                bias_uv(0)
                split_x(1)
                split_qk_high(1)
                split_qk_low(1)
                step(0, older=False, root=False)
                step(1, root=False)
                with dve.Fori(0, BATCH // 2 - 2) as i:
                    own.enter(i, OWN_PER_PAIR)
                    step(i * 2 + 2)
                    step(i * 2 + 3)
                own.leave(BATCH // 2 - 2)
                step(BATCH - 2, newer=1)
                step(BATCH - 1, newer=0)
                b = BATCH - 1
                copy_heads(b, 1)
                gate(b, 0)
                gate(b, 1)
                z_stats(b)
                root()
                add_y(b - 1)
                z_sums()
                z_centre()
                z_variance()
                root_seed()
                copy_yt(b)
                root()
                copy_y(b)
                add_y(b)
                own.settle()

            dve.wait_ge(made, MADE)
            ffn(0)
            attention()
            ffn(1)


INPUTS = ["L0_attn_x", "L0_attn_W1", "L0_attn_b1", "L0_attn_W2", "L0_attn_b2", "L0_attn_gamma", "L0_attn_beta",
          "L0_ffn_router_w", "L0_ffn_router_b", "L0_ffn_w1", "L0_ffn_b1", "L0_ffn_w2", "L0_ffn_b2"]


def kernel(**inputs):
    import concourse.bacc as bacc
    from concourse.bass_utils import run_bass_kernel_spmd

    nc = bacc.Bacc("TRN2", target_bir_lowering=False, num_devices=1)
    arrays, args = {}, []
    for name in INPUTS:
        a = np.ascontiguousarray(inputs[name])
        if name == "L0_attn_x":
            a = a.reshape(TOKENS, D)
        arrays[f"in_{name}"] = a
        args.append(nc.dram_tensor(f"in_{name}", a.shape, mybir.dt.from_np(a.dtype), kind="ExternalInput").ap())
    args.append(nc.dram_tensor("out", (TOKENS, D), F32, kind="ExternalOutput").ap())
    macaron(nc, *args)
    result = run_bass_kernel_spmd(nc, [arrays], core_ids=[0])
    return result.results[0]["out"].reshape(BATCH, SEQ, D)
```

```python
from contextlib import ExitStack

import numpy as np

import concourse.bass as bass
from concourse import mybir

F32 = mybir.dt.float32
F32R = mybir.dt.float32r
F16 = mybir.dt.float16
BF16 = mybir.dt.bfloat16
I32 = mybir.dt.int32
U32 = mybir.dt.uint32
ALU = mybir.AluOpType
ACT = mybir.ActivationFunctionType
AX = mybir.AxisListType

P = 128
D = 128
BATCH, SEQ = 8, 256
TOKENS = BATCH * SEQ
TILES = TOKENS // P
TPB = SEQ // P
HEADS, HD = 16, 8
HG = 4
GROUPS = HEADS // HG
REP = 4
EXPERTS, FF = 8, 512
CHUNKS = FF // P
TOPK = 2
SLOT_TILES = (TOPK * TOKENS + EXPERTS * (P - 1)) // P
MAP_STEP = 8
RING = 4
LAST = (SLOT_TILES - 1) // RING
BACK = [slice(0, 4), slice(4, 8), slice(8, 12), slice(12, 14), slice(14, 16)]
AHEAD = 5
V_STEP = HG * 32 + HD
EPS = 1e-5
RSQRT_SEED = 0x5F3759DF
NEWTON = 3
C_W1, C_W2, C_B1, C_B2 = 0, FF, 2 * FF, 2 * FF + CHUNKS
RECORD = C_B2 + D


class Steps:

    def __init__(self, engine, semaphore):
        self.engine, self.semaphore, self.count, self.turn = engine, semaphore, 0, 0

    def mark(self, instruction):
        instruction.then_inc(self.semaphore, 1)
        self.count += 1

    def settle(self):
        self.engine.wait_ge(self.semaphore, self.turn + self.count)

    def done(self, instruction):
        self.mark(instruction)
        self.settle()

    def enter(self, i, per_turn):
        self.turn, self.start, self.per_turn = i * per_turn, self.count, per_turn

    def leave(self, turns):
        assert self.count - self.start == self.per_turn, (self.count - self.start, self.per_turn)
        self.count, self.turn = self.start + turns * self.per_turn, 0


def turns(k):
    return (SLOT_TILES - k + RING - 1) // RING


def exists(s):
    return not isinstance(s, int) or s < SLOT_TILES


def wait(engine, semaphore, value):
    if not isinstance(value, int) or value > 0:
        engine.wait_ge(semaphore, value)


def macaron(nc, x, W1, b1, W2, b2, gamma, beta, router_w, router_b, w1, fb1, w2, fb2, out):
    ctx = ExitStack()
    with ctx:
        def sb(name, shape, dt=F32):
            return ctx.enter_context(nc.sbuf_tensor(name, shape, dt))

        def sem(name):
            return ctx.enter_context(nc.semaphore(name))

        xn_rows = nc.dram_tensor("xn_rows", [TOKENS, D], F32).ap()
        y_rows = nc.dram_tensor("y_rows", [TOPK * TOKENS + SLOT_TILES * P, D], F32).ap()

        ident = sb("ident", [P, P])
        ones = sb("ones", [P, P])
        ones_h = sb("ones_h", [P, P], BF16)
        before = sb("before", [P, P], BF16)
        iota = sb("iota", [P, P])
        token_id = sb("token_id", [P, TILES])
        rank_of = sb("rank_of", [P, EXPERTS])
        spare_row = sb("spare_row", [P, SLOT_TILES])
        quarter = sb("quarter", [P, HG])
        table_out = sb("table_out", [P, 1])
        ones8 = sb("ones8", [P, EXPERTS])
        records = sb("records", [P, EXPERTS, RECORD])
        row = sb("row", [1, EXPERTS * D + EXPERTS + 2 * D + D])
        rw = sb("rw", [P, EXPERTS])
        rb_all = sb("rb_all", [P, EXPERTS])
        rw_sum = sb("rw_sum", [P, EXPERTS])
        uvb_all = sb("uvb_all", [P, 2 * D])
        w_in = sb("w_in", [P, 4 * D])
        w_in_hi = sb("w_in_hi", [P, 4 * D], F32R)
        w_in_lo = sb("w_in_lo", [P, 4 * D], F32R)
        w_out = sb("w_out", [P, D])
        w_out_g = sb("w_out_g", [P, D])
        cols = sb("cols", [P, 6])
        beta_all = sb("beta_all", [P, P])
        yb_all = sb("yb_all", [P, D])
        spread = sb("spread", [P, 4, GROUPS, P], F32R)

        X = sb("X", [P, TILES, D])
        stats = sb("stats", [P, TILES, 6])
        mean = sb("mean", [P, TILES])
        rstd = sb("rstd", [P, TILES])
        shift = sb("shift", [P, TILES])
        work = [sb(f"work{i}", [P, TILES]) for i in range(4)]

        LG = sb("LG", [P, TILES, EXPERTS])
        one_hot = sb("one_hot", [P, TOPK, TILES, EXPERTS])
        weighed = sb("weighed", [P, TILES, EXPERTS])
        chosen_place = sb("chosen_place", [P, TOPK, TILES, EXPERTS])
        top = sb("top", [P, TOPK, TILES])
        first = sb("first", [P, TILES])
        half_gate = sb("half_gate", [P, TOPK, TILES])
        chosen = sb("chosen", [P, TILES, EXPERTS], BF16)
        running = sb("running", [P, 1 + EXPERTS * TILES])
        place = sb("place", [P, EXPERTS, TILES])
        n_int = sb("n_int", [P, EXPERTS], I32)
        n_tiles = sb("n_tiles", [P, EXPERTS])
        n_upto = sb("n_upto", [P, EXPERTS])
        base = sb("base", [P, EXPERTS])
        te_cmp = sb("te_cmp", [1, SLOT_TILES, EXPERTS])
        te_sum = sb("te_sum", [1, SLOT_TILES])
        tile_expert = sb("tile_expert", [1, SLOT_TILES], I32)
        slot_i = sb("slot_i", [P, TOPK * TILES], I32)
        slot_f = sb("slot_f", [P, TOPK * TILES])
        slot_lo_i = sb("slot_lo_i", [P, TOPK * TILES], I32)
        slot_hi_i = sb("slot_hi_i", [P, TOPK * TILES], I32)
        region = sb("region", [P, TILES * TOPK * D])
        YL = region[:].rearrange("p (t j d) -> p t j d", j=TOPK, d=D)
        A = region[:].rearrange("p (n j q) -> p n j q", j=HG, q=SEQ)
        halves, N = region[:].bitcast(F16), TOPK * TILES
        in_tile = halves[:, 0:N * P].rearrange("p (n s) -> p n s", n=N)
        tile_hot = halves[:, N * P:N * (P + SLOT_TILES)].rearrange("p (n s) -> p n s", n=N)
        tile_load = halves[:, N * (P + SLOT_TILES):N * (P + 3 * SLOT_TILES)].rearrange(
            "p (n a s) -> p n a s", n=N, a=2)
        dst_f = sb("dst_f", [P, SLOT_TILES])
        src_row = sb("src_row", [P, SLOT_TILES], U32)
        dst_row = sb("dst_row", [P, SLOT_TILES], U32)

        src_s = [sb(f"src_s{k}", [P, 1], U32) for k in range(RING)]
        dst_s = [sb(f"dst_s{k}", [P, 1], U32) for k in range(RING)]
        XG = sb("XG", [P, RING, D])
        XT = sb("XT", [P, RING, P])
        WB = sb("WB", [P, RING, RECORD])
        HT = sb("HT", [P, 2, CHUNKS, P])
        YG = sb("YG", [P, RING, D])

        XTr = HT[:].rearrange("p a c q -> p a (c q)")

        XA = sb("XA", [P, TPB, D])
        xt_hi = sb("xt_hi", [P, SEQ], F32R)
        xt_lo = sb("xt_lo", [P, SEQ], F32R)
        QK = sb("QK", [P, 2, SEQ])
        qk_hi = sb("qk_hi", [P, 2, SEQ], F32R)
        qk_lo = sb("qk_lo", [P, 2, SEQ], F32R)
        uv_pre = sb("uv_pre", [P, TPB, 2 * D])
        U = sb("U", [P, TILES, D])
        XN = U
        VP = sb("VP", [P, 2, TPB, GROUPS * V_STEP])
        KS = sb("KS", [P, 2, GROUPS, SEQ], F32R)
        QS = sb("QS", [P, GROUPS, SEQ])
        QM = sb("QM", [P, 2, GROUPS, HG, SEQ], F32R)
        AT = sb("AT", [P, SEQ])
        Z = sb("Z", [P, TPB, D])
        YT = sb("YT", [P, TPB, P])
        zst = sb("zst", [P, TPB, 6])
        z_sum = sb("z_sum", [P, TPB])
        z_diff = sb("z_diff", [P, TPB])
        z_var = sb("z_var", [P, TPB])
        z_half = sb("z_half", [P, TPB])
        z_step = sb("z_step", [P, TPB])
        z_rstd = sb("z_rstd", [P, TPB])
        Y = sb("Y", [P, TPB, D])
        PS = ctx.enter_context(nc.psum_tensor("PS", [P, 8, 512], F32))

        names = """made passed loaded router_in  bias_ps bias_out set_up spread_zero dve_own
            xn_ready x_t_ps x_t_out logits_ps tops_diff exp_top chosen_made counts_ps
            hot_made token_load load_made map_ps src_staged xg_t_ps xt_ready w_staged up_ps gelu_out down_ps y_ready
            dst_staged x_first y_scaled x_out x_final ln_ready xn_attn xa_ready x_biased
            xt_ps xt_split qk_ps qk_act uv_ps uv_biased uv_act qk_split rep_ps rep_out qm_ready
            s_ps s_act av_ps at_out z_ps z_gated z_centred yt_ps yt_out y_ps y_out stored stored_xn""".split()
        S = {n: sem(n) for n in names}
        gathered = [sem(f"gathered{k}") for k in range(RING)]
        scattered = [sem(f"scattered{k}") for k in range(RING)]
        y_back = [sem(f"y_back{k}") for k in range(len(BACK))]
        w_loads = [sem(f"w_loads{k}") for k in range(2)]
        x_in = [sem(f"x_in{k}") for k in range(4)]
        made, loaded, bias_ps, bias_out, set_up, spread_zero, router_in = (
            S[n] for n in ("made", "loaded", "bias_ps", "bias_out", "set_up", "spread_zero", "router_in"))

        LOADS = 9
        MADE = 15
        x_t = x.rearrange("(t p) d -> p t d", p=P)
        out_t = out.rearrange("(t p) d -> p t d", p=P)
        R_B2, R_RB, R_UV, R_YB = 0, EXPERTS * D, EXPERTS * D + EXPERTS, EXPERTS * D + EXPERTS + 2 * D
        OWN_PER_PAIR = 2 * 17
        QTR = TILES // 4

        block = ctx.enter_context(nc.Block())

        @block.sync
        def _(sp):
            sp.dma_start(X[:, 0:QTR, :], x_t[:, 0:QTR, :]).then_inc(x_in[0], 16)
            for k in range(1, 4):
                sp.dma_start(X[:, k * QTR:(k + 1) * QTR, :], x_t[:, k * QTR:(k + 1) * QTR, :]).then_inc(x_in[k], 16)
            sp.dma_start(row[:, R_B2:R_RB], fb2.rearrange("(a e) d -> a (e d)", a=1)).then_inc(loaded, 16)
            sp.dma_start(row[:, R_UV:R_YB], b1[0:2 * D].rearrange("(a e) -> a e", a=1)).then_inc(loaded, 16)
            sp.dma_start(row[:, R_YB:R_YB + D], b2.rearrange("(a e) -> a e", a=1)).then_inc(loaded, 16)
            sp.dma_start(cols[:, 0:1], gamma.rearrange("(p a) -> p a", a=1)).then_inc(loaded, 16)
            sp.dma_start(cols[:, 1:2], beta.rearrange("(p a) -> p a", a=1)).then_inc(loaded, 16)
            for c in (2, 3):
                sp.dma_start(cols[:, 2 + c:3 + c],
                              b1[c * D:(c + 1) * D].rearrange("(p a) -> p a", a=1)).then_inc(loaded, 16)
            sp.dma_start(w_in[:], W1).then_inc(loaded, 16)
            sp.dma_start(w_out[:], W2).then_inc(loaded, 16)
            sp.wait_ge(loaded, 16 * LOADS)
            sp.dma_start(records[:, :, C_B1:C_B2], fb1.rearrange("e (p c) -> p e c", p=P)).then_inc(w_loads[0], 16)
            sp.dma_start(records[:, :, C_W1:C_W2], w1.rearrange("e d f -> d e f")).then_inc(w_loads[0], 16)
            sp.dma_start(records[:, :, C_W2:C_B1], w2.rearrange("e (p c) d -> p e (c d)", p=P)).then_inc(w_loads[1], 16)

            def ffn(f):
                for c in range(4):
                    sp.wait_ge(S["xn_ready"], 4 * f + c + 1)
                    sp.dma_start(xn_rows[c * QTR * P:(c + 1) * QTR * P, :].rearrange("(t p) d -> p t d", p=P),
                                 XN[:, c * QTR:(c + 1) * QTR, :]).then_inc(S["stored_xn"], 16)
                for k in range(RING):
                    sp.wait_ge(scattered[k], 16 * (f + 1) * turns(k))
                for q, back in zip(BACK, y_back):
                    rows = y_rows[q.start * P * TOPK:q.stop * P * TOPK, :]
                    sp.dma_start(YL[:, q, :, :],
                                 rows.rearrange("(t p j) d -> p t j d", p=P, j=TOPK)).then_inc(back, 16)

            ffn(0)
            ffn(1)
            for c, q in enumerate(BACK):
                sp.wait_ge(S["x_out"], len(BACK) + c + 1)
                sp.dma_start(out_t[:, q, :], X[:, q, :]).then_inc(S["stored"], 16)
            sp.wait_ge(S["stored"], 16 * len(BACK))

        @block.gpsimd
        def _(pool):
            def make(ins):
                ins.then_inc(made, 1)

            make(pool.memset(ident[:], 0.0))
            make(pool.memset(before[:], 1.0))
            make(pool.memset(ones[:], 1.0))
            make(pool.memset(ones_h[:], 1.0))
            make(pool.memset(quarter[:], 1.0))
            make(pool.memset(ones8[:], 1.0))
            make(pool.iota(iota[:], pattern=[[1, P]], base=0, channel_multiplier=0,
                           allow_small_or_imprecise_dtypes=True))
            make(pool.iota(token_id[:], pattern=[[P, TILES]], base=0, channel_multiplier=1,
                           allow_small_or_imprecise_dtypes=True))
            make(pool.iota(rank_of[:], pattern=[[-1, EXPERTS]], base=EXPERTS, channel_multiplier=0,
                           allow_small_or_imprecise_dtypes=True))
            make(pool.iota(spare_row[:], pattern=[[P, SLOT_TILES]], base=TOPK * TOKENS + 1, channel_multiplier=1,
                           allow_small_or_imprecise_dtypes=True))
            make(pool.memset(running[:, 0:1], 0.0))
            pool.wait_ge(made, 11)
            make(pool.affine_select(out=ident[:], in_=ident[:], compare_op=ALU.not_equal, fill=1.0, base=0,
                                    pattern=[[-1, P]], channel_multiplier=1))
            make(pool.affine_select(out=before[:], in_=before[:], compare_op=ALU.is_gt, fill=0.0, base=0,
                                    pattern=[[1, P]], channel_multiplier=-1))
            make(pool.affine_select(out=quarter[:], in_=quarter[:], compare_op=ALU.is_ge, fill=0.0, base=0,
                                    pattern=[[-32, HG]], channel_multiplier=1))
            pool.wait_ge(made, MADE - 1)
            make(pool.affine_select(out=quarter[:], in_=quarter[:], compare_op=ALU.is_ge, fill=0.0, base=31,
                                    pattern=[[32, HG]], channel_multiplier=-1))
            pool.memset(VP[:], 0.0)
            pool.memset(spread[:].bitcast(F32), 0.0).then_inc(spread_zero, 1)
            pool.wait_ge(loaded, 16 * LOADS)
            pool.tensor_copy(beta_all[:], cols[:, 1:2].to_broadcast([P, P])).then_inc(set_up, 1)
            pool.tensor_scalar(w_out_g[:], w_out[:], cols[:, 0:1], 1.0, ALU.mult, ALU.mult).then_inc(set_up, 1)
            pool.tensor_copy(w_in_hi[:], w_in[:]).then_inc(set_up, 1)
            pool.wait_ge(set_up, 3)
            pool.tensor_tensor(w_in_lo[:], w_in[:], w_in_hi[:].bitcast(F32), ALU.subtract).then_inc(set_up, 1)
            pool.wait_ge(spread_zero, 1)
            pool.wait_ge(made, MADE)
            picks = ident[:].rearrange("p (j g d) -> p g j d", g=GROUPS, d=HD)
            for part, copies in enumerate(((0, 1), (2, 3), (0, 2), (1, 3))):
                to = spread[:, part, :, :].rearrange("p g (j r d) -> p g j r d", r=REP, d=HD)
                for r in copies:
                    last = pool.tensor_copy(to[:, :, :, r, :], picks)
            last.then_inc(set_up, 1)

            def ffn(f):
                n0 = f * SLOT_TILES

                def gather(s, k):
                    pool.wait_ge(S["src_staged"], s + (n0 + 1))
                    pool.sem_inc(S["passed"], 1)
                    pool.indirect_dma_start(XG[:, k, :], None, xn_rows,
                                            bass.IndirectOffsetOnAxis(ap=src_s[k][:], axis=0)).then_inc(gathered[k], 16)

                def scatter(s, k):
                    pool.wait_ge(S["y_ready"], s + (n0 + 1))
                    pool.sem_inc(S["passed"], 1)
                    pool.indirect_dma_start(y_rows, bass.IndirectOffsetOnAxis(ap=dst_s[k][:], axis=0),
                                            YG[:, k, :], None).then_inc(scattered[k], 16)

                def group(g):
                    for k in range(RING):
                        s = g * RING + k
                        if exists(s + AHEAD):
                            gather(s + AHEAD, (k + AHEAD) % RING)
                        if exists(s):
                            scatter(s, k)

                for j in range(TOPK):
                    q = slice(j * TILES, (j + 1) * TILES)
                    pool.wait_ge(S["hot_made"], TOPK * f + j + 1)
                    pool.tensor_tensor(tile_load[:, q, 0, :], tile_hot[:, q, :],
                                       token_id[:].unsqueeze(2).to_broadcast([P, TILES, SLOT_TILES]), ALU.mult
                                       ).then_inc(S["token_load"], 1)
                pool.wait_ge(S["stored_xn"], 64 * (f + 1))
                for s in range(AHEAD):
                    gather(s, s % RING)
                group(0)
                with pool.Fori(1, LAST - 1) as g:
                    group(g)
                group(LAST - 1)
                group(LAST)
                for c, q in enumerate(BACK):
                    if f == 0 and c == 2:
                        pool.wait_ge(S["xn_attn"], 1)
                        prepare(0)
                    pool.wait_ge(S["x_first"], len(BACK) * f + c + 1)
                    pool.wait_ge(S["y_scaled"], len(BACK) * f + c + 1)
                    pool.tensor_tensor(X[:, q, :], X[:, q, :], YL[:, q, 1, :], ALU.add).then_inc(S["x_out"], 1)

            def masks(b, par):
                for r in range(2):
                    pool.wait_ge(S["rep_out"], b * 4 + (r + 1))
                    if r == 0:
                        wait(pool, S["s_ps"], (b - 1) * 8)
                    pool.sem_inc(S["passed"], 1)
                    for j in range(HG):
                        last = pool.tensor_scalar(QM[:, par, 2 * r:2 * r + 2, j, :], QS[:, 2 * r:2 * r + 2, :],
                                                  quarter[:, j:j + 1], 1.0, ALU.mult, ALU.mult)
                    last.then_inc(S["qm_ready"], 1)

            def prepare(b):
                wait(pool, S["xt_ps"], b)
                pool.sem_inc(S["passed"], 1)
                pool.tensor_copy(XA[:], XN[:, bass.ds(b * TPB, TPB), :]).then_inc(S["xa_ready"], 1)

            ffn(0)
            pool.wait_ge(S["xn_attn"], 2)
            prepare(1)
            masks(0, 0)
            pool.wait_ge(S["xn_attn"], 3)
            prepare(2)
            masks(1, 1)
            pool.wait_ge(S["xn_attn"], 4)
            pool.tensor_tensor(X[:], X[:], yb_all[:].unsqueeze(1).to_broadcast([P, TILES, D]), ALU.add
                               ).then_inc(S["x_biased"], 1)
            with pool.Fori(1, BATCH // 2 - 1) as i:
                prepare(i * 2 + 1)
                masks(i * 2, 0)
                prepare(i * 2 + 2)
                masks(i * 2 + 1, 1)
            prepare(BATCH - 1)
            masks(BATCH - 2, 0)
            masks(BATCH - 1, 1)
            ffn(1)

        @block.tensor
        def _(pe):
            def keep_warm(n, bank=3):
                for _ in range(n):
                    pe.matmul(PS[:, bank, 0:P], ones[:], ones[:], start=True, stop=True)

            def keep_warm(n, bank=3):
                for _ in range(n):
                    pe.matmul(PS[:, bank, 0:P], ones[:], ones[:], start=True, stop=True)

            pe.wait_ge(made, 3)
            keep_warm(9, bank=7)
            pe.wait_ge(made, MADE)

            pe.wait_ge(router_in, 32)
            pe.matmul(PS[:, 2, 0:EXPERTS], ones[0:1, :], row[:, R_RB:R_UV], start=True, stop=True)
            pe.matmul(PS[:, 2, EXPERTS:2 * EXPERTS], ones[:], rw[:], start=True, stop=True).then_inc(bias_ps, 1)

            def biases():
                pe.wait_ge(loaded, 16 * LOADS)
                pe.wait_ge(S["x_t_out"], 4)
                for h in range(2):
                    pe.matmul(PS[:, h, :], ones[0:1, :], row[:, 512 * h:512 * h + 512],
                              start=True, stop=True).then_inc(bias_ps, 1)
                pe.wait_ge(bias_out, 1)
                pe.matmul(PS[:, 2, 0:2 * D], ones[0:1, :], row[:, R_UV:R_YB], start=True, stop=True)
                pe.wait_ge(set_up, 1)
                pe.matmul(PS[:, 2, 2 * D:3 * D], beta_all[:], w_out[:], start=True, stop=False)
                pe.matmul(PS[:, 2, 2 * D:3 * D], ones[0:1, :], row[:, R_YB:R_YB + D], start=False, stop=True
                          ).then_inc(bias_ps, 1)

            def turn_rows(f, c):
                if f == 0:
                    pe.wait_ge(x_in[c], 16)
                else:
                    pe.wait_ge(S["x_final"], 1 if c < 3 else 2)
                wait(pe, S["x_t_out"], 4 * f + c - 1)
                for k in range(QTR):
                    mm = pe.transpose(PS[:, c % 2, k * P:(k + 1) * P], X[:, c * QTR + k, :], ident[:])
                mm.then_inc(S["x_t_ps"], 1)

            def router_products(f, c):
                pe.wait_ge(S["x_t_out"], 4 * f + c + 1)
                for k in range(QTR):
                    t = c * QTR + k
                    mm = pe.matmul(PS[:, 3, t * EXPERTS:(t + 1) * EXPERTS], XTr[:, c % 2, k * P:(k + 1) * P], rw[:],
                                   start=True, stop=True)
                mm.then_inc(S["logits_ps"], 1)

            def ffn(f):
                n0 = f * SLOT_TILES
                if f == 0:
                    turn_rows(0, 0)
                    for c in range(3):
                        turn_rows(0, c + 1)
                        keep_warm(2, bank=7)
                        router_products(0, c)
                    router_products(0, 3)
                    biases()
                else:
                    turn_rows(1, 3)
                    router_products(1, 3)
                pe.wait_ge(S["chosen_made"], f + 1)
                every = chosen[:].rearrange("p t e -> p e t")
                pe.matmul(PS[:, 6, 0:P], before[:], every, start=True, stop=True)
                pe.matmul(PS[:, 7, 0:P], ones_h[:], every, start=True, stop=True).then_inc(S["counts_ps"], 1)
                keep_warm(24)
                for n in range(TOPK * TILES):
                    if n % TILES == 0:
                        pe.wait_ge(S["token_load"], TOPK * f + n // TILES + 1)
                    if n % MAP_STEP == 0:
                        pe.wait_ge(S["load_made"], (TOPK * TILES * f + n) // MAP_STEP + 1)
                    mm = pe.matmul(PS[:, 5, 0:2 * SLOT_TILES], in_tile[:, n, :],
                                   tile_load[:, n, :, :].rearrange("p a s -> p (a s)"),
                                   start=(n == 0), stop=(n == TOPK * TILES - 1))
                mm.then_inc(S["map_ps"], 1)
                keep_warm(12)

                if f == 0:
                    pe.wait_ge(bias_out, 5)

                def turn(s, k, g):
                    pe.wait_ge(gathered[k], (g + (f * turns(k) + 1)) * 16)
                    wait(pe, S["xt_ready"], s + (n0 - 1))
                    pe.transpose(PS[:, k % 2, 0:P], XG[:, k, :], ident[:]).then_inc(S["xg_t_ps"], 1)

                def up(s, k):
                    pe.wait_ge(S["xt_ready"], s + (n0 + 1))
                    pe.wait_ge(S["w_staged"], s + (n0 + 1))
                    wait(pe, S["gelu_out"], (s + (n0 - 1)) * CHUNKS)
                    for c in range(CHUNKS):
                        mm = pe.matmul(PS[:, 2 + k % 2, c * P:(c + 1) * P], WB[:, k, C_W1 + c:C_W1 + FF:CHUNKS],
                                       XT[:, k, :], start=True, stop=True)
                    mm.then_inc(S["up_ps"], 1)

                def down(s, k):
                    wait(pe, S["y_ready"], s + (n0 - 1))
                    for c in range(CHUNKS):
                        pe.wait_ge(S["gelu_out"], (s + n0) * CHUNKS + (c + 1))
                        mm = pe.matmul(PS[:, 4 + k % 2, 0:D], HT[:, k % 2, c, :],
                                       WB[:, k, C_W2 + c * D:C_W2 + (c + 1) * D],
                                       start=(c == 0), stop=(c == CHUNKS - 1))
                    mm.then_inc(S["down_ps"], 1)

                def group(g):
                    for k in range(RING):
                        s = g * RING + k
                        if exists(s + 2):
                            turn(s + 2, (k + 2) % RING, g + (k + 2) // RING)
                        if exists(s + 1):
                            up(s + 1, (k + 1) % RING)
                        if exists(s):
                            down(s, k)

                turn(0, 0, 0)
                turn(1, 1, 0)
                up(0, 0)
                group(0)
                with pe.Fori(1, LAST) as g:
                    group(g)
                group(LAST)

            def project(b, part):
                if part == "turn":
                    pe.wait_ge(S["xa_ready"], b + 1)
                    wait(pe, S["rep_out"], 4 * (b - 1) + 3)
                    for t in range(TPB):
                        mm = pe.transpose(PS[:, 5, t * P:(t + 1) * P], XA[:, t, :], ident[:])
                    mm.then_inc(S["xt_ps"], 1)
                elif part == "qk":
                    pe.wait_ge(S["xt_split"], b + 1)
                    wait(pe, S["rep_out"], 4 * b)
                    for c in range(2):
                        q = slice((2 + c) * D, (3 + c) * D)
                        for n, (w, m) in enumerate(((w_in_hi, xt_hi), (w_in_hi, xt_lo), (w_in_lo, xt_hi))):
                            mm = pe.matmul(PS[:, 4, c * SEQ:(c + 1) * SEQ], w[:, q], m[:], start=(n == 0), stop=(n == 2))
                    mm.then_inc(S["qk_ps"], 1)
                else:
                    pe.wait_ge(S["rep_out"], b * 4 + 1)
                    for t in range(TPB):
                        q = slice(t * P, (t + 1) * P)
                        for n, (m, w) in enumerate(((xt_hi, w_in_hi), (xt_lo, w_in_hi), (xt_hi, w_in_lo))):
                            mm = pe.matmul(PS[:, 4, t * 2 * D:(t + 1) * 2 * D], m[:, q], w[:, 0:2 * D],
                                           start=(n == 0), stop=(n == 2))
                    mm.then_inc(S["uv_ps"], 1)

            def replicate(b, r):
                c, bank = r // 2, (4, 5, 5, 4)[r]
                if r == 0:
                    pe.wait_ge(S["qk_split"], b + 1)
                elif r == 2:
                    pe.wait_ge(S["rep_out"], b * 4 + 2)
                elif r == 3:
                    pe.wait_ge(S["uv_biased"], b + 1)
                for h in range(2):
                    g = 2 * (r % 2) + h
                    pe.matmul(PS[:, bank, h * SEQ:(h + 1) * SEQ], spread[:, 2 * c, g, :], qk_hi[:, c, :],
                              start=True, stop=False)
                    mm = pe.matmul(PS[:, bank, h * SEQ:(h + 1) * SEQ], spread[:, 2 * c + 1, g, :], qk_lo[:, c, :],
                                   start=False, stop=True)
                mm.then_inc(S["rep_ps"], 1)

            def scores(b, par, n):
                g, kt = n // 2, n % 2
                if n % 4 == 0:
                    pe.wait_ge(S["qm_ready"], b * 2 + (n // 4 + 1))
                    pe.wait_ge(S["rep_out"], b * 4 + (n // 4 + 3))
                wait(pe, S["s_act"], b * 8 + (n - 1))
                for h in range(2):
                    mm = pe.matmul(PS[:, 2 * (n % 2) + h, :], KS[:, par, g, kt * P:(kt + 1) * P],
                                   QM[:, par, g, 2 * h:2 * h + 2, :].rearrange("p j q -> p (j q)"),
                                   start=True, stop=True)
                mm.then_inc(S["s_ps"], 1)

            def attend(b, par, g):
                if g == 0:
                    pe.wait_ge(S["uv_act"], b + 1)
                    wait(pe, S["at_out"], b)
                pe.wait_ge(S["s_act"], b * 8 + (2 * g + 2))
                for kt in range(TPB):
                    for j in range(HG):
                        h = (HG * g + j) * 32
                        mm = pe.matmul(PS[32 * j:32 * j + 32, 6, 0:SEQ],
                                       VP[:, par, kt, h:h + 32], A[:, (2 * g + kt) % 4, j, :],
                                       start=(g == 0 and kt == 0), stop=(g == GROUPS - 1 and kt == TPB - 1),
                                       tile_position=(0, 32 * j))
                mm.then_inc(S["av_ps"], 1)

            def back(b):
                pe.wait_ge(S["at_out"], b + 1)
                wait(pe, S["y_out"], b)
                for t in range(TPB):
                    mm = pe.transpose(PS[:, 7, t * P:(t + 1) * P], AT[:, t * P:(t + 1) * P], ident[:])
                mm.then_inc(S["z_ps"], 1)

            def output(b, part):
                if part == "turn":
                    pe.wait_ge(S["z_centred"], b + 1)
                    for t in range(TPB):
                        mm = pe.transpose(PS[:, 7, t * P:(t + 1) * P], Z[:, t, :], ident[:])
                    mm.then_inc(S["yt_ps"], 1)
                else:
                    pe.wait_ge(S["yt_out"], b + 1)
                    for t in range(TPB):
                        mm = pe.matmul(PS[:, 7, t * D:(t + 1) * D], YT[:, t, :], w_out_g[:], start=True, stop=True)
                    mm.then_inc(S["y_ps"], 1)

            def step(b, par, older=True, newer=2, first=False):
                scores(b, par, 0)
                scores(b, par, 1)
                if first:
                    project(b + 1, "qk")
                    keep_warm(4, bank=7)
                if older:
                    attend(b - 1, 1 - par, 3)
                scores(b, par, 2)
                if newer and not first:
                    replicate(b + 1, 0)
                attend(b, par, 0)
                if first:
                    replicate(b + 1, 0)
                if older:
                    back(b - 1)
                scores(b, par, 3)
                if newer:
                    replicate(b + 1, 1)
                scores(b, par, 4)
                if newer:
                    project(b + 1, "uv")
                attend(b, par, 1)
                if newer:
                    replicate(b + 1, 2)
                scores(b, par, 5)
                if newer:
                    replicate(b + 1, 3)
                if newer > 1:
                    project(b + 2, "turn")
                if older:
                    output(b - 1, "turn")
                scores(b, par, 6)
                attend(b, par, 2)
                if older:
                    output(b - 1, "out")
                scores(b, par, 7)
                if newer > 1:
                    project(b + 2, "qk")

            def attention():
                pe.wait_ge(S["y_ready"], SLOT_TILES)
                pe.wait_ge(S["gelu_out"], SLOT_TILES * CHUNKS)
                pe.wait_ge(set_up, 5)
                pe.wait_ge(S["x_out"], 2)
                keep_warm(8)
                project(0, "turn")
                project(0, "qk")
                keep_warm(6)
                replicate(0, 0)
                replicate(0, 1)
                project(0, "uv")
                replicate(0, 2)
                replicate(0, 3)
                project(1, "turn")
                step(0, 0, older=False, first=True)
                step(1, 1)
                with pe.Fori(1, BATCH // 2 - 1) as i:
                    step(i * 2, 0)
                    step(i * 2 + 1, 1)
                step(BATCH - 2, 0, newer=1)
                step(BATCH - 1, 1, newer=0)
                b = BATCH - 1
                attend(b, 1, 3)
                pe.wait_ge(S["s_act"], 8 * BATCH)
                turn_rows(1, 0)
                back(b)
                turn_rows(1, 1)
                router_products(1, 0)
                turn_rows(1, 2)
                output(b, "turn")
                router_products(1, 1)
                output(b, "out")
                router_products(1, 2)

            ffn(0)
            attention()
            ffn(1)

        @block.scalar
        def _(act):
            act.dma_start(rw[:], router_w).then_inc(router_in, 16)
            act.dma_start(row[:, R_RB:R_UV], router_b.rearrange("(a e) -> a e", a=1)).then_inc(router_in, 16)
            act.wait_ge(bias_ps, 1)
            act.copy(rb_all[:], PS[:, 2, 0:EXPERTS])
            act.copy(rw_sum[:], PS[:, 2, EXPERTS:2 * EXPERTS]).then_inc(bias_out, 1)

            def load_table(function):
                act.activation(table_out[:], quarter[:, 0:1], function)

            def ffn(f):
                n0 = f * SLOT_TILES
                for c in range(4):
                    act.wait_ge(S["x_t_ps"], 4 * f + c + 1)
                    wait(act, S["logits_ps"], 4 * f + c - 1)
                    act.copy(XTr[:, c % 2, :], PS[:, c % 2, :]).then_inc(S["x_t_out"], 1)

                def copy_biases():
                    for h in range(2):
                        act.wait_ge(bias_ps, h + 2)
                        act.copy(records[:, 4 * h:4 * h + 4, C_B2:RECORD],
                                 PS[:, h, :].rearrange("p (e d) -> p e d", d=D)).then_inc(bias_out, 1)
                    act.wait_ge(bias_ps, 4)
                    act.copy(uvb_all[:], PS[:, 2, 0:2 * D]).then_inc(bias_out, 1)
                    act.copy(yb_all[:], PS[:, 2, 2 * D:3 * D]).then_inc(bias_out, 1)
                act.wait_ge(S["ln_ready"], f + 1)
                for c in range(4):
                    for t in range(c * QTR, (c + 1) * QTR):
                        a = act.activation(XN[:, t, :], X[:, t, :], ACT.Identity, scale=rstd[:, t:t + 1],
                                           bias=shift[:, t:t + 1])
                    a.then_inc(S["xn_ready"], 1)
                act.wait_ge(S["tops_diff"], f + 1)
                act.activation(work[1][:], work[0][:], ACT.Exp).then_inc(S["exp_top"], 1)
                if f == 0:
                    copy_biases()
                load_table(ACT.Gelu)

                def gelu(s, k):
                    wait(act, S["down_ps"], s + (n0 - 1))
                    act.wait_ge(S["up_ps"], s + (n0 + 1))
                    for c in range(CHUNKS):
                        act.activation(HT[:, k % 2, c, :], PS[:, 2 + k % 2, c * P:(c + 1) * P], ACT.Gelu,
                                       bias=WB[:, k, C_B1 + c:C_B1 + c + 1]).then_inc(S["gelu_out"], 1)

                for k in range(RING):
                    gelu(k, k)
                with act.Fori(1, LAST) as g:
                    for k in range(RING):
                        gelu(g * RING + k, k)
                for k in range(SLOT_TILES - LAST * RING):
                    gelu(LAST * RING + k, k)
                for q, back in zip(BACK, y_back):
                    act.wait_ge(back, (f + 1) * 16)
                    for t in range(q.start, q.stop):
                        a = act.activation(YL[:, t, 1, :], YL[:, t, 1, :], ACT.Copy, scale=half_gate[:, 1, t:t + 1])
                    a.then_inc(S["y_scaled"], 1)

            def silu_scores(b, n):
                act.wait_ge(S["s_ps"], b * 8 + (n + 1))
                if n % 2 == 0:
                    wait(act, S["av_ps"], b * 4 + (n // 2 - 1))
                act.activation(A[:, n % 4, :, :].rearrange("p j q -> p (j q)"),
                               PS[:, 2 * (n % 2):2 * (n % 2) + 2, :].rearrange("p a q -> p (a q)"),
                               ACT.Silu).then_inc(S["s_act"], 1)

            def silu_qk(b):
                act.wait_ge(S["qk_ps"], b + 1)
                wait(act, S["qk_split"], b)
                for c in range(2):
                    a = act.activation(QK[:, c, :], PS[:, 4, c * SEQ:(c + 1) * SEQ], ACT.Silu, bias=cols[:, 4 + c:5 + c])
                a.then_inc(S["qk_act"], 1)

            def silu_uv(b, par):
                act.wait_ge(S["uv_biased"], b + 1)
                wait(act, S["av_ps"], (b - 1) * 4)
                act.activation(U[:, bass.ds(b * TPB, TPB), :], uv_pre[:, :, 0:D], ACT.Silu)
                for t in range(TPB):
                    to = VP[:, par, t, :].rearrange("p (g s) -> p g s", s=V_STEP)[:, :, 0:HG * 32]
                    a = act.activation(to.rearrange("p g (j r) -> p g j r", r=32)[:, :, :, 0:HD],
                                       uv_pre[:, t, D:2 * D].rearrange("p (j g r) -> p g j r", j=HG, r=HD), ACT.Silu)
                a.then_inc(S["uv_act"], 1)

            def copy_keys(b, par, r):
                act.wait_ge(S["rep_ps"], b * 4 + (r + 1))
                wait(act, S["s_ps"], (b - 1) * 8)
                act.copy(KS[:, par, 2 * (r - 2):2 * (r - 1), :],
                         PS[:, 7 - r, :].rearrange("p (g q) -> p g q", g=2)).then_inc(S["rep_out"], 1)

            def step(b, par, newer=2, first=False):
                for n in range(5):
                    silu_scores(b, n)
                    if first and n == 1:
                        silu_qk(b + 1)
                if newer:
                    copy_keys(b + 1, 1 - par, 2)
                silu_scores(b, 5)
                if newer:
                    copy_keys(b + 1, 1 - par, 3)
                silu_scores(b, 6)
                if newer:
                    silu_uv(b + 1, 1 - par)
                silu_scores(b, 7)
                if newer > 1:
                    silu_qk(b + 2)

            ffn(0)
            silu_qk(0)
            copy_keys(0, 0, 2)
            copy_keys(0, 0, 3)
            silu_uv(0, 0)
            step(0, 0, first=True)
            step(1, 1)
            with act.Fori(1, BATCH // 2 - 1) as i:
                step(i * 2, 0)
                step(i * 2 + 1, 1)
            step(BATCH - 2, 0, newer=1)
            step(BATCH - 1, 1, newer=0)
            ffn(1)

        @block.vector
        def _(dve):
            own = Steps(dve, S["dve_own"])
            link = own.done

            def ln_coefficients(st, mu, rs, w):
                dve.tensor_tensor(w[1], st[:, :, 2], st[:, :, 5], ALU.add)
                dve.tensor_tensor(mu, st[:, :, 1], st[:, :, 4], ALU.add)
                link(dve.tensor_tensor(w[0], st[:, :, 1], st[:, :, 4], ALU.subtract))
                dve.tensor_scalar(w[1], w[1], 1.0 / D, EPS, ALU.mult, ALU.add)
                dve.tensor_scalar(mu, mu, 0.5, None, ALU.mult)
                link(dve.scalar_tensor_tensor(out=w[0], in0=w[0], scalar=0.25, in1=w[0], op0=ALU.mult, op1=ALU.mult))
                link(dve.tensor_tensor(w[1], w[1], w[0], ALU.add))
                dve.tensor_scalar(w[3], w[1], -0.5, None, ALU.mult)
                link(dve.tensor_scalar(rs.bitcast(I32), w[1].bitcast(I32), -0.5, float(RSQRT_SEED), ALU.mult, ALU.add))
                for _ in range(NEWTON):
                    link(dve.tensor_tensor(w[2], rs, rs, ALU.mult))
                    link(dve.tensor_tensor(w[2], w[2], w[3], ALU.mult))
                    link(dve.scalar_tensor_tensor(out=rs, in0=w[2], scalar=1.5, in1=rs, op0=ALU.add, op1=ALU.mult))

            def tile_stats(t):
                return dve.bn_stats(stats[:, t, :], X[:, t, :])

            def chunk_stats(c):
                dve.wait_ge(S["x_out"], c + 1)
                for t in range(BACK[c].start, BACK[c].stop):
                    n = tile_stats(t)
                return n

            def coefficients(lo=0, hi=TILES):
                ln_coefficients(stats[:, lo:hi, :], mean[:, lo:hi], rstd[:, lo:hi], [w[:, lo:hi] for w in work])

            def normalize_rows(first_t, end_t):
                for t in range(first_t, end_t):
                    n = dve.tensor_scalar(XN[:, t, :], X[:, t, :], mean[:, t:t + 1], rstd[:, t:t + 1],
                                          ALU.subtract, ALU.mult)
                n.then_inc(S["xn_attn"], 1)

            def ffn(f):
                n0 = f * SLOT_TILES
                if f == 0:
                    for t in range(TILES):
                        if t % QTR == 0:
                            dve.wait_ge(x_in[t // QTR], 16)
                        n = tile_stats(t)
                    link(n)
                coefficients()
                dve.scalar_tensor_tensor(out=shift[:], in0=mean[:], scalar=-1.0, in1=rstd[:], op0=ALU.mult,
                                         op1=ALU.mult).then_inc(S["ln_ready"], 1)
                if f == 0:
                    dve.wait_ge(made, MADE)
                dve.wait_ge(S["ln_ready"], f + 1)
                dve.wait_ge(S["logits_ps"], 4 * (f + 1))
                if f == 0:
                    dve.wait_ge(bias_out, 1)
                by_tile = [P, TILES, EXPERTS]
                dve.tensor_tensor(LG[:], PS[:, 3, 0:TILES * EXPERTS].rearrange("p (t e) -> p t e", e=EXPERTS),
                                  rstd[:].unsqueeze(2).to_broadcast(by_tile), ALU.mult)
                link(dve.tensor_tensor(weighed[:], rw_sum[:].unsqueeze(1).to_broadcast(by_tile),
                                       shift[:].unsqueeze(2).to_broadcast(by_tile), ALU.mult))
                link(dve.tensor_tensor(weighed[:], weighed[:], rb_all[:].unsqueeze(1).to_broadcast(by_tile), ALU.add))
                link(dve.tensor_tensor(LG[:], LG[:], weighed[:], ALU.add))
                ranks = rank_of[:].unsqueeze(1).to_broadcast([P, TILES, EXPERTS])
                for j in range(TOPK):
                    link(dve.tensor_reduce(top[:, j, :], LG[:], AX.X, ALU.max))
                    link(dve.tensor_tensor(weighed[:], LG[:],
                                           top[:, j, :].unsqueeze(2).to_broadcast([P, TILES, EXPERTS]), ALU.is_equal))
                    link(dve.tensor_tensor(weighed[:], weighed[:], ranks, ALU.mult))
                    link(dve.tensor_reduce(first[:], weighed[:], AX.X, ALU.max))
                    link(dve.tensor_tensor(one_hot[:, j, :, :], ranks,
                                           first[:].unsqueeze(2).to_broadcast([P, TILES, EXPERTS]), ALU.is_equal))
                    if j == 0:
                        link(dve.scalar_tensor_tensor(out=LG[:], in0=one_hot[:, 0, :, :], scalar=-3.0e38, in1=LG[:],
                                                      op0=ALU.mult, op1=ALU.add))
                dve.tensor_tensor(work[0][:], top[:, 1, :], top[:, 0, :], ALU.subtract).then_inc(S["tops_diff"], 1)
                dve.tensor_tensor(chosen[:], one_hot[:, 0, :, :], one_hot[:, 1, :, :], ALU.add).then_inc(S["chosen_made"], 1)
                dve.wait_ge(S["counts_ps"], f + 1)
                link(dve.tensor_tensor_scan(running[:, 1:], ones[:], PS[:, 7, 0:P], 0.0, ALU.mult, ALU.add))
                upto = running[:, 1:].rearrange("p (e t) -> p e t", t=TILES)
                earlier = running[:, 0:EXPERTS * TILES].rearrange("p (e t) -> p e t", t=TILES)
                ahead = PS[:, 6, 0:P].rearrange("p (e t) -> p e t", t=TILES)
                dve.tensor_tensor(place[:], earlier, ahead, ALU.add)
                link(dve.scalar_tensor_tensor(out=n_int[:], in0=upto[:, :, TILES - 1], scalar=float(P - 1),
                                              in1=earlier[:, :, 0], op0=ALU.add, op1=ALU.subtract))
                link(dve.tensor_scalar(n_int[:], n_int[:], 7, None, ALU.logical_shift_right))
                link(dve.tensor_copy(n_tiles[:], n_int[:]))
                link(dve.tensor_tensor_scan(n_upto[:], ones8[:], n_tiles[:], 0.0, ALU.mult, ALU.add))
                link(dve.tensor_tensor(base[:], n_upto[:], n_tiles[:], ALU.subtract))
                link(dve.scalar_tensor_tensor(out=base[:], in0=base[:], scalar=float(P), in1=earlier[:, :, 0],
                                              op0=ALU.mult, op1=ALU.subtract))
                link(dve.tensor_tensor(place[:], place[:], base[:].unsqueeze(2).to_broadcast([P, EXPERTS, TILES]), ALU.add))
                link(dve.tensor_tensor(chosen_place[:], one_hot[:], place[:].rearrange("p e t -> p t e").unsqueeze(1)
                                       .to_broadcast([P, TOPK, TILES, EXPERTS]), ALU.mult))
                link(dve.tensor_reduce(slot_f[:], chosen_place[:].rearrange("p j t e -> p (j t) e"), AX.X, ALU.add))
                link(dve.tensor_copy(slot_i[:], slot_f[:]))
                dve.tensor_scalar(slot_lo_i[:], slot_i[:], P - 1, None, ALU.bitwise_and)
                link(dve.tensor_scalar(slot_hi_i[:], slot_i[:], 7, None, ALU.logical_shift_right))
                N = TOPK * TILES
                for j in range(TOPK):
                    q = slice(j * TILES, (j + 1) * TILES)
                    shape = [P, TILES, SLOT_TILES]
                    dve.tensor_tensor(tile_hot[:, q, :], iota[:, 0:SLOT_TILES].unsqueeze(1).to_broadcast(shape),
                                      slot_hi_i[:, q].unsqueeze(2).to_broadcast(shape), ALU.is_equal
                                      ).then_inc(S["hot_made"], 1)
                for j in range(TOPK):
                    q = slice(j * TILES, (j + 1) * TILES)
                    dve.wait_ge(S["hot_made"], TOPK * f + j + 1)
                    dve.tensor_scalar(tile_load[:, q, 1, :], tile_hot[:, q, :], float(j + 1), None, ALU.mult)
                    for n in range(j * TILES, (j + 1) * TILES, MAP_STEP):
                        q = slice(n, n + MAP_STEP)
                        dve.tensor_tensor(in_tile[:, q, :], iota[:].unsqueeze(1).to_broadcast([P, MAP_STEP, P]),
                                          slot_lo_i[:, q].unsqueeze(2).to_broadcast([P, MAP_STEP, P]), ALU.is_equal
                                          ).then_inc(S["load_made"], 1)
                dve.wait_ge(S["map_ps"], f + 1)
                token, choice = (PS[:, 5, a * SLOT_TILES:(a + 1) * SLOT_TILES] for a in range(2))
                link(dve.tensor_copy(src_row[:], token))

                def gates():
                    dve.wait_ge(S["exp_top"], f + 1)
                    link(dve.tensor_scalar(work[2][:], work[1][:], 1.0, None, ALU.add))
                    link(dve.reciprocal(work[3][:], work[2][:]))
                    link(dve.tensor_scalar(half_gate[:, 0, :], work[3][:], 0.5, None, ALU.mult))
                    link(dve.tensor_tensor(half_gate[:, 1, :], half_gate[:, 0, :], work[1][:], ALU.mult))

                def slot_tile_experts():
                    every = [1, SLOT_TILES, EXPERTS]
                    link(dve.tensor_tensor(te_cmp[:], iota[0:1, 0:SLOT_TILES].unsqueeze(2).to_broadcast(every),
                                           n_upto[0:1, :].unsqueeze(1).to_broadcast(every), ALU.is_ge))
                    link(dve.tensor_reduce(te_sum[:], te_cmp[:], AX.X, ALU.add))
                    link(dve.tensor_scalar(tile_expert[:], te_sum[:], float(EXPERTS - 1), None, ALU.min))

                def rows_to_write():
                    link(dve.tensor_scalar(dst_f[:], choice, 0.0, None, ALU.is_equal))
                    link(dve.tensor_tensor(dst_f[:], dst_f[:], spare_row[:], ALU.mult))
                    link(dve.scalar_tensor_tensor(out=dst_f[:], in0=dst_f[:], scalar=-1.0, in1=choice,
                                                  op0=ALU.add, op1=ALU.add))
                    link(dve.scalar_tensor_tensor(out=dst_row[:], in0=token, scalar=float(TOPK), in1=dst_f[:],
                                                  op0=ALU.mult, op1=ALU.add))

                def stage_src(s, k):
                    wait(dve, S["xg_t_ps"], s + (n0 - 3))
                    dve.tensor_copy(src_s[k][:], src_row[:, bass.ds(s, 1)]).then_inc(S["src_staged"], 1)

                def stage_weights(s, k):
                    wait(dve, S["y_ready"], s + (n0 - 3))
                    e = dve.value_load(tile_expert[0:1, bass.ds(s, 1)], min_val=0, max_val=EXPERTS - 1)
                    dve.tensor_copy(WB[:, k, :], records[:, bass.ds(e, 1), :].rearrange("p a r -> p (a r)")
                                    ).then_inc(S["w_staged"], 1)

                def evacuate_x(s, k):
                    dve.wait_ge(S["xg_t_ps"], s + (n0 + 1))
                    wait(dve, S["up_ps"], s + (n0 - 3))
                    dve.tensor_copy(XT[:, k, :], PS[:, k % 2, 0:P]).then_inc(S["xt_ready"], 1)

                def evacuate_y(s, k, g):
                    wait(dve, scattered[k], (g + f * turns(k)) * 16)
                    dve.tensor_copy(dst_s[k][:], dst_row[:, bass.ds(s, 1)]).then_inc(S["dst_staged"], 1)
                    dve.wait_ge(S["down_ps"], s + (n0 + 1))
                    dve.wait_ge(S["w_staged"], s + (n0 + 1))
                    dve.tensor_tensor(YG[:, k, :], PS[:, 4 + k % 2, 0:D], WB[:, k, C_B2:RECORD], ALU.add
                                      ).then_inc(S["y_ready"], 1)

                def group(g):
                    for k in range(RING):
                        s = g * RING + k
                        if exists(s + AHEAD):
                            stage_src(s + AHEAD, (k + AHEAD) % RING)
                        if exists(s + 2):
                            evacuate_x(s + 2, (k + 2) % RING)
                        if exists(s):
                            evacuate_y(s, k, g)
                        if exists(s + 3):
                            stage_weights(s + 3, (k + 3) % RING)

                for s in range(RING):
                    stage_src(s, s)
                slot_tile_experts()
                if f == 0:
                    for k in range(2):
                        dve.wait_ge(w_loads[k], 32 - 16 * k)
                    dve.wait_ge(bias_out, 5)
                stage_weights(0, 0)
                rows_to_write()
                stage_weights(1, 1)
                evacuate_x(0, 0)
                stage_src(RING, 0)
                stage_weights(2, 2)
                evacuate_x(1, 1)
                gates()
                group(0)
                with dve.Fori(1, LAST - 1) as g:
                    group(g)
                group(LAST - 1)
                group(LAST)
                if f == 0:
                    dve.wait_ge(loaded, 16 * LOADS)
                for c, q in enumerate(BACK):
                    dve.wait_ge(y_back[c], (f + 1) * 16)
                    for t in range(q.start, q.stop):
                        n = dve.scalar_tensor_tensor(out=X[:, t, :], in0=YL[:, t, 0, :], scalar=half_gate[:, 0, t:t + 1],
                                                     in1=X[:, t, :], op0=ALU.mult, op1=ALU.add)
                    n.then_inc(S["x_first"], 1)
                    if f == 0 and c == 1:
                        link(chunk_stats(0))
                        coefficients(0, QTR)
                        normalize_rows(0, TPB)

            def split_x(b):
                dve.wait_ge(S["xt_ps"], b + 1)
                wait(dve, S["uv_ps"], b)
                link(dve.tensor_copy(xt_hi[:], PS[:, 5, 0:SEQ]))
                dve.tensor_tensor(xt_lo[:], PS[:, 5, 0:SEQ], xt_hi[:].bitcast(F32), ALU.subtract).then_inc(S["xt_split"], 1)

            def split_qk_high(b):
                dve.wait_ge(S["qk_act"], b + 1)
                wait(dve, S["rep_ps"], b * 4)
                own.mark(dve.tensor_copy(qk_hi[:], QK[:]))

            def split_qk_low(b):
                own.settle()
                dve.tensor_tensor(qk_lo[:], QK[:], qk_hi[:].bitcast(F32), ALU.subtract).then_inc(S["qk_split"], 1)

            def bias_uv(b):
                dve.wait_ge(S["uv_ps"], b + 1)
                wait(dve, S["uv_act"], b)
                dve.tensor_tensor(uv_pre[:], PS[:, 4, :].rearrange("p (t d) -> p t d", t=TPB),
                                  uvb_all[:].unsqueeze(1).to_broadcast([P, TPB, 2 * D]), ALU.add).then_inc(S["uv_biased"], 1)

            def copy_queries(b, r):
                dve.wait_ge(S["rep_ps"], b * 4 + (r + 1))
                wait(dve, S["qm_ready"], b * 2 + (r - 1))
                dve.tensor_copy(QS[:, 2 * r:2 * r + 2, :], PS[:, 4 + r, :].rearrange("p (g q) -> p g q", g=2)
                                ).then_inc(S["rep_out"], 1)

            def copy_heads(b):
                dve.wait_ge(S["av_ps"], b * 4 + 4)
                wait(dve, S["z_ps"], b)
                dve.tensor_copy(AT[:], PS[:, 6, 0:SEQ]).then_inc(S["at_out"], 1)

            def gate(b):
                dve.wait_ge(S["z_ps"], b + 1)
                wait(dve, S["yt_ps"], b)
                dve.scalar_tensor_tensor(out=Z[:], in0=PS[:, 7, 0:TPB * D].rearrange("p (t d) -> p t d", t=TPB),
                                         scalar=0.5 / SEQ, in1=U[:, bass.ds(b * TPB, TPB), :],
                                         op0=ALU.mult, op1=ALU.mult).then_inc(S["z_gated"], 1)

            def z_stats(b):
                dve.wait_ge(S["z_gated"], b + 1)
                for t in range(TPB):
                    n = dve.bn_stats(zst[:, t, :], Z[:, t, :])
                own.mark(n)

            def z_sums():
                own.settle()
                dve.tensor_tensor(z_diff[:], zst[:, :, 1], zst[:, :, 4], ALU.subtract)
                dve.tensor_tensor(z_var[:], zst[:, :, 2], zst[:, :, 5], ALU.add)
                own.mark(dve.tensor_tensor(z_sum[:], zst[:, :, 1], zst[:, :, 4], ALU.add))

            def z_centre():
                own.settle()
                for t in range(TPB):
                    n = dve.tensor_scalar(Z[:, t, :], Z[:, t, :], 2.0, z_sum[:, t:t + 1], ALU.mult, ALU.subtract)
                n.then_inc(S["z_centred"], 1)
                dve.tensor_scalar(z_var[:], z_var[:], 4.0 / D, EPS, ALU.mult, ALU.add)
                own.mark(dve.tensor_tensor(z_diff[:], z_diff[:], z_diff[:], ALU.mult))

            def z_variance():
                own.settle()
                own.mark(dve.tensor_tensor(z_var[:], z_var[:], z_diff[:], ALU.add))

            def root_seed():
                own.settle()
                dve.tensor_scalar(z_half[:], z_var[:], -0.5, None, ALU.mult)
                own.mark(dve.tensor_scalar(z_rstd[:].bitcast(I32), z_var[:].bitcast(I32), -0.5, float(RSQRT_SEED),
                                           ALU.mult, ALU.add))

            def root_square():
                own.settle()
                own.mark(dve.tensor_tensor(z_step[:], z_rstd[:], z_rstd[:], ALU.mult))

            def root_scale():
                own.settle()
                own.mark(dve.tensor_tensor(z_step[:], z_step[:], z_half[:], ALU.mult))

            def root_refine():
                own.settle()
                own.mark(dve.scalar_tensor_tensor(out=z_rstd[:], in0=z_step[:], scalar=1.5, in1=z_rstd[:],
                                                  op0=ALU.add, op1=ALU.mult))

            def copy_yt(b):
                dve.wait_ge(S["yt_ps"], b + 1)
                wait(dve, S["y_ps"], b)
                dve.tensor_copy(YT[:], PS[:, 7, 0:SEQ].rearrange("p (t d) -> p t d", t=TPB)).then_inc(S["yt_out"], 1)

            def copy_y(b):
                dve.wait_ge(S["y_ps"], b + 1)
                dve.tensor_copy(Y[:], PS[:, 7, 0:TPB * D].rearrange("p (t d) -> p t d", t=TPB)).then_inc(S["y_out"], 1)

            def add_y(b):
                own.settle()
                dve.wait_ge(S["y_out"], b + 1)
                dve.wait_ge(S["x_biased"], 1)
                for t in range(TPB):
                    xt = X[:, bass.ds(b * TPB + t, 1), :].rearrange("p a d -> p (a d)")
                    n = dve.scalar_tensor_tensor(out=xt, in0=Y[:, t, :], scalar=z_rstd[:, t:t + 1], in1=xt,
                                                 op0=ALU.mult, op1=ALU.add)
                own.mark(n)

            def step(b, older=True, newer=2, root=True, first=False):
                if older:
                    copy_heads(b - 1)
                if root:
                    root_square()
                if newer:
                    copy_queries(b + 1, 0)
                if root:
                    root_scale()
                if older:
                    gate(b - 1)
                if root:
                    root_refine()
                if older:
                    z_stats(b - 1)
                if root:
                    root_square()
                if newer:
                    copy_queries(b + 1, 1)
                if root:
                    root_scale()
                if older:
                    z_sums()
                if root:
                    root_refine()
                if newer:
                    bias_uv(b + 1)
                if first:
                    normalize_rows(QTR + TPB, TILES)
                if root:
                    root_square()
                if older:
                    z_centre()
                if root:
                    root_scale()
                if newer > 1:
                    split_x(b + 2)
                if root:
                    root_refine()
                if older:
                    z_variance()
                    copy_yt(b - 1)
                if root:
                    add_y(b - 2)
                if older:
                    root_seed()
                    copy_y(b - 1)
                if newer > 1:
                    split_qk_high(b + 2)
                    split_qk_low(b + 2)

            def root():
                for _ in range(NEWTON):
                    root_square()
                    root_scale()
                    root_refine()

            def attention():
                split_x(0)
                chunk_stats(1)
                chunk_stats(2)
                split_qk_high(0)
                split_qk_low(0)
                normalize_rows(TPB, QTR)
                for c in range(3, len(BACK)):
                    n = chunk_stats(c)
                copy_queries(0, 0)
                copy_queries(0, 1)
                bias_uv(0)
                link(n)
                split_x(1)
                coefficients(QTR, TILES)
                split_qk_high(1)
                split_qk_low(1)
                normalize_rows(QTR, QTR + TPB)
                step(0, older=False, root=False, first=True)
                step(1, root=False)
                with dve.Fori(0, BATCH // 2 - 2) as i:
                    own.enter(i, OWN_PER_PAIR)
                    step(i * 2 + 2)
                    step(i * 2 + 3)
                own.leave(BATCH // 2 - 2)
                step(BATCH - 2, newer=1)
                step(BATCH - 1, newer=0)
                b = BATCH - 1
                root()
                add_y(b - 1)
                own.settle()
                dve.sem_inc(S["x_final"], 1)
                copy_heads(b)
                for t in range(4):
                    tile_stats(t)
                gate(b)
                z_stats(b)
                tile_stats(4)
                z_sums()
                tile_stats(5)
                z_centre()
                z_variance()
                tile_stats(6)
                copy_yt(b)
                root_seed()
                for n in range(NEWTON):
                    root_square()
                    tile_stats(7 + 2 * n)
                    root_scale()
                    tile_stats(8 + 2 * n)
                    root_refine()
                tile_stats(7 + 2 * NEWTON)
                copy_y(b)
                add_y(b)
                own.settle()
                dve.sem_inc(S["x_final"], 1)
                for t in range(8 + 2 * NEWTON, TILES):
                    n = tile_stats(t)
                link(n)

            ffn(0)
            attention()
            ffn(1)


INPUTS = ["L0_attn_x", "L0_attn_W1", "L0_attn_b1", "L0_attn_W2", "L0_attn_b2", "L0_attn_gamma", "L0_attn_beta",
          "L0_ffn_router_w", "L0_ffn_router_b", "L0_ffn_w1", "L0_ffn_b1", "L0_ffn_w2", "L0_ffn_b2"]


def kernel(**inputs):
    import concourse.bacc as bacc
    from concourse.bass_utils import run_bass_kernel_spmd

    nc = bacc.Bacc("TRN2", target_bir_lowering=False, num_devices=1)
    arrays, args = {}, []
    for name in INPUTS:
        a = np.ascontiguousarray(inputs[name])
        if name == "L0_attn_x":
            a = a.reshape(TOKENS, D)
        arrays[f"in_{name}"] = a
        args.append(nc.dram_tensor(f"in_{name}", a.shape, mybir.dt.from_np(a.dtype), kind="ExternalInput").ap())
    args.append(nc.dram_tensor("out", (TOKENS, D), F32, kind="ExternalOutput").ap())
    macaron(nc, *args)
    result = run_bass_kernel_spmd(nc, [arrays], core_ids=[0])
    return result.results[0]["out"].reshape(BATCH, SEQ, D)
```
